# Optimizing a Trainium2 kernel written in Bass

```python
import numpy as np
import jax
import jax.numpy as jnp

def _softmax(x, axis=-1):
    return jax.nn.softmax(x, axis=axis)

def _gelu(x):
    return jax.nn.gelu(x, approximate=True)

def _silu(x):
    return jax.nn.silu(x)

def _sigmoid(x):
    return jax.nn.sigmoid(x)

def _layernorm(x, axis=-1, eps=1e-05):
    m = jnp.mean(x, axis=axis, keepdims=True)
    v = jnp.var(x, axis=axis, keepdims=True)
    return (x - m) / jnp.sqrt(v + eps)

def _scatter_add(tgt, idx, src, axis=0):
    return tgt.at[idx].add(src)

def _segment_sum(src, seg, n):
    return jax.ops.segment_sum(src, seg, n)
kernel_name = 'mk_xattn_seq_d1_seqx_r4_f74cc1'

def setup_inputs(seed: int=0):
    np.random.seed(seed)
    _w = jnp.asarray

    def _rec_inputs():
        import jax
        import jax.numpy as jnp
        _rk = jax.random.key(seed)
        x = 7.22e-05 + 1 * jax.random.normal(jax.random.fold_in(_rk, 1), (128, 128, 256), jnp.float32)
        _lenS = 128 - jax.random.randint(jax.random.fold_in(_rk, 7), (128,), 0, max(1, 128 // 4) + 1, jnp.int32)
        _lenS2 = 128 - jax.random.randint(jax.random.fold_in(_rk, 8), (128,), 0, max(1, 128 // 4) + 1, jnp.int32)
        _ctx_1024P = jax.random.normal(jax.random.fold_in(_rk, 11), (128, 16, 256), jnp.float32)
        _ctx_1024c = jax.random.dirichlet(jax.random.fold_in(_rk, 511), 0.3 * jnp.ones((16,), jnp.float32), (128, 128))
        _ctx_1024t = jnp.einsum('bsk,bkd->bsd', _ctx_1024c, _ctx_1024P)
        _ctx_1024t = _ctx_1024t * jax.lax.rsqrt(jnp.mean(jnp.square(_ctx_1024t)) + 1e-12) * 0.953939
        ctx_1024 = 4.13588e-05 + 0.999923 * (_ctx_1024t + 0.3 * jax.random.normal(jax.random.fold_in(_rk, 611), (128, 128, 256), jnp.float32))
        _validS = jnp.arange(128)[None, :] < _lenS[:, None]
        _validS2 = jnp.arange(128)[None, :] < _lenS2[:, None]
        _causal = jnp.tril(jnp.ones((128, 128), dtype=bool))
        mask_BxSxS2_fk0 = jnp.where(jnp.broadcast_to(_validS2[:, None, :], (128, 128, 128)), 0.0, 1.0).astype(jnp.float32)
        return (x, ctx_1024, mask_BxSxS2_fk0)
    x, ctx_1024, mask_BxSxS2_fk0 = _rec_inputs()

    def _L0_xattn_setup():
        import jax, jax.numpy as jnp
        import numpy as np
        import math
        B, S, D, H, FF = (4, 512, 256, 16, 1024)
        HD = D // H
        EPS = 1e-05

        def _layer_norm(x, g, b):
            m = jnp.mean(x, axis=-1, keepdims=True)
            v = jnp.mean((x - m) ** 2, axis=-1, keepdims=True)
            return (x - m) * jax.lax.rsqrt(v + EPS) * g + b

        def _self_attn(x, mask, Wq, bq, Wk, bk, Wv, bv, Wo, bo):
            b, s, d = x.shape
            q = (x @ Wq.T + bq).reshape(b, s, H, HD)
            k = (x @ Wk.T + bk).reshape(b, s, H, HD)
            v = (x @ Wv.T + bv).reshape(b, s, H, HD)
            score = jnp.einsum('bshd,bthd->bhst', q, k) / math.sqrt(HD)
            score = score + (1.0 - mask[:, None, :, :]) * -1000000000.0
            p = jax.nn.softmax(score, axis=-1)
            o = jnp.einsum('bhst,bthd->bshd', p, v).reshape(b, s, d)
            return o @ Wo.T + bo
        key = jax.random.key(seed)
        ks = jax.random.split(key, 16)
        sd = 0.02
        inp = {'tgt': jax.random.normal(ks[0], (B, S, D), jnp.float32), 'memory': jax.random.normal(ks[1], (B, S, D), jnp.float32), 'mask': jnp.broadcast_to(jnp.tril(jnp.ones((S, S), jnp.float32)), (B, S, S)), 'Wq': jax.random.normal(ks[2], (D, D), jnp.float32) * sd, 'bq': jnp.zeros((D,), jnp.float32), 'Wk': jax.random.normal(ks[3], (D, D), jnp.float32) * sd, 'bk': jnp.zeros((D,), jnp.float32), 'Wv': jax.random.normal(ks[4], (D, D), jnp.float32) * sd, 'bv': jnp.zeros((D,), jnp.float32), 'Wo': jax.random.normal(ks[5], (D, D), jnp.float32) * sd, 'bo': jnp.zeros((D,), jnp.float32), 'Wg': jax.random.normal(ks[6], (D, D), jnp.float32) * sd, 'bg': jnp.zeros((D,), jnp.float32), 'W1': jax.random.normal(ks[7], (FF, D), jnp.float32) * sd, 'b1': jnp.zeros((FF,), jnp.float32), 'W2': jax.random.normal(ks[8], (D, FF), jnp.float32) * sd, 'b2': jnp.zeros((D,), jnp.float32), 'g1': jnp.ones((D,), jnp.float32), 'be1': jnp.zeros((D,), jnp.float32), 'g2': jnp.ones((D,), jnp.float32), 'be2': jnp.zeros((D,), jnp.float32)}
        return inp
    _L0_xattn_all = _L0_xattn_setup()
    _L0_xattn_in = {k: v for k, v in _L0_xattn_all.items() if k in ('Wq', 'bq', 'Wk', 'bk', 'Wv', 'bv', 'Wo', 'bo', 'Wg', 'bg', 'W1', 'b1', 'W2', 'b2', 'g1', 'be1', 'g2', 'be2')}
    del _L0_xattn_all
    return {'x': x, 'ctx_1024': ctx_1024, 'mask_BxSxS2_fk0': mask_BxSxS2_fk0, 'L0_xattn_Wq': _L0_xattn_in['Wq'], 'L0_xattn_bq': _L0_xattn_in['bq'], 'L0_xattn_Wk': _L0_xattn_in['Wk'], 'L0_xattn_bk': _L0_xattn_in['bk'], 'L0_xattn_Wv': _L0_xattn_in['Wv'], 'L0_xattn_bv': _L0_xattn_in['bv'], 'L0_xattn_Wo': _L0_xattn_in['Wo'], 'L0_xattn_bo': _L0_xattn_in['bo'], 'L0_xattn_Wg': _L0_xattn_in['Wg'], 'L0_xattn_bg': _L0_xattn_in['bg'], 'L0_xattn_W1': _L0_xattn_in['W1'], 'L0_xattn_b1': _L0_xattn_in['b1'], 'L0_xattn_W2': _L0_xattn_in['W2'], 'L0_xattn_b2': _L0_xattn_in['b2'], 'L0_xattn_g1': _L0_xattn_in['g1'], 'L0_xattn_be1': _L0_xattn_in['be1'], 'L0_xattn_g2': _L0_xattn_in['g2'], 'L0_xattn_be2': _L0_xattn_in['be2']}

def reference(x, ctx_1024, mask_BxSxS2_fk0, L0_xattn_Wq, L0_xattn_bq, L0_xattn_Wk, L0_xattn_bk, L0_xattn_Wv, L0_xattn_bv, L0_xattn_Wo, L0_xattn_bo, L0_xattn_Wg, L0_xattn_bg, L0_xattn_W1, L0_xattn_b1, L0_xattn_W2, L0_xattn_b2, L0_xattn_g1, L0_xattn_be1, L0_xattn_g2, L0_xattn_be2):
    import jax
    import jax.numpy as jnp

    def _L0_xattn_ref(tgt, memory, mask, Wq, bq, Wk, bk, Wv, bv, Wo, bo, Wg, bg, W1, b1, W2, b2, g1, be1, g2, be2):
        import jax, jax.numpy as jnp
        import numpy as np
        import math
        B, S, D, H, FF = (4, 512, 256, 16, 1024)
        HD = D // H
        EPS = 1e-05

        def _layer_norm(x, g, b):
            m = jnp.mean(x, axis=-1, keepdims=True)
            v = jnp.mean((x - m) ** 2, axis=-1, keepdims=True)
            return (x - m) * jax.lax.rsqrt(v + EPS) * g + b

        def _self_attn(x, mask, Wq, bq, Wk, bk, Wv, bv, Wo, bo):
            b, s, d = x.shape
            q = (x @ Wq.T + bq).reshape(b, s, H, HD)
            k = (x @ Wk.T + bk).reshape(b, s, H, HD)
            v = (x @ Wv.T + bv).reshape(b, s, H, HD)
            score = jnp.einsum('bshd,bthd->bhst', q, k) / math.sqrt(HD)
            score = score + (1.0 - mask[:, None, :, :]) * -1000000000.0
            p = jax.nn.softmax(score, axis=-1)
            o = jnp.einsum('bhst,bthd->bshd', p, v).reshape(b, s, d)
            return o @ Wo.T + bo
        tgt1 = _layer_norm(tgt, g1, be1)
        tgt = tgt + _self_attn(tgt1, mask, Wq, bq, Wk, bk, Wv, bv, Wo, bo)
        tgt = tgt + (memory @ Wg.T + bg)
        tgt1 = _layer_norm(tgt, g2, be2)
        ff = jax.nn.relu(tgt1 @ W1.T + b1) @ W2.T + b2
        return tgt + ff
    x = _L0_xattn_ref(x, ctx_1024, mask_BxSxS2_fk0, L0_xattn_Wq, L0_xattn_bq, L0_xattn_Wk, L0_xattn_bk, L0_xattn_Wv, L0_xattn_bv, L0_xattn_Wo, L0_xattn_bo, L0_xattn_Wg, L0_xattn_bg, L0_xattn_W1, L0_xattn_b1, L0_xattn_W2, L0_xattn_b2, L0_xattn_g1, L0_xattn_be1, L0_xattn_g2, L0_xattn_be2)
    return x

_drawn_inputs = setup_inputs


def setup_inputs(seed=0):
    import zlib

    import numpy as np

    out = dict(_drawn_inputs(seed))
    spreads = {'L0_xattn_bq': (0.0, 0.8),
     'L0_xattn_bk': (0.0, 0.8),
     'L0_xattn_bv': (0.0, 0.1),
     'L0_xattn_bo': (0.0, 0.1),
     'L0_xattn_bg': (0.0, 0.1),
     'L0_xattn_b1': (0.0, 0.1),
     'L0_xattn_b2': (0.0, 0.1),
     'L0_xattn_g1': (1.0, 0.6),
     'L0_xattn_be1': (0.0, 0.8),
     'L0_xattn_g2': (1.0, 0.6),
     'L0_xattn_be2': (0.0, 0.591)}
    factors = {'L0_xattn_Wq': 8.0, 'L0_xattn_Wk': 8.0}
    for name, (base, spread) in spreads.items():
        noise = np.random.default_rng([zlib.crc32(name.encode()), seed]).standard_normal(out[name].shape)
        drawn = base * np.exp(spread * noise) if base else spread * noise
        out[name] = jnp.asarray(drawn.astype(out[name].dtype))
    for name, factor in factors.items():
        out[name] = (out[name] * factor).astype(out[name].dtype)
    return out
```

```python
from contextlib import ExitStack

import concourse.bass as bass
from concourse import mybir

ALU = mybir.AluOpType
ACT = mybir.ActivationFunctionType
F32 = mybir.dt.float32
F32R = mybir.dt.float32r
I32 = mybir.dt.int32

P = 128
EPS = 1e-5
MASKED = 1e9
LOWEST = -3.0e38
RSQRT_SEED = float(0x5F3759DF)
NEWTON_STEPS = 3

TICKS = 13
TURN_LAG = 3
DOWN_TICKS = (7, 8, 10, 11)
VALUE_LAG = 5


def later(g):
    return not (isinstance(g, int) and g == 0)


def head_of(c, h):
    return 8 * (h // 2) + 2 * c + h % 2


def xattn_block(nc, x, memory, mask, wqT, wkT, wvT, woT, wgT, w1T, w2T,
                bq, bk, bv, bo, bg, b1, b2, g1, be1, g2, be2, identity, parity, out):
    B, S, D = x.shape
    FF = w1T.shape[1]
    H = 16
    HD = D // H
    GB = 2
    GROUPS = B // GB
    ROWS = GB * S
    KT = D // P
    FT = FF // P
    CH = 4
    CPB = H // CH
    CHUNKS = GB * CPB
    HJ = FT // 2
    SLOT = 32
    assert S == P and D == 2 * P and CHUNKS == 8 and HJ == 4

    x_rows = x.rearrange("(g b) s d -> g s b d", b=GB)
    mem_rows = memory.rearrange("(g b) s d -> g s b d", b=GB)
    mask_rows = mask.rearrange("(g b) s t -> g s b t", b=GB)
    out_rows = out.rearrange("(g b) s d -> g s b d", b=GB)

    with ExitStack() as ctx:
        def sb(name, shape, dt=F32):
            return ctx.enter_context(nc.sbuf_tensor(name, shape, dt))

        def bank(name):
            return ctx.enter_context(nc.psum_tensor(name, [P, 512], F32))

        def sem(name):
            return ctx.enter_context(nc.semaphore(name))

        ident = sb("ident", [P, P])
        par = sb("par", [P, 2])
        g1c, be1c = sb("g1c", [P, KT]), sb("be1c", [P, KT])
        g2c, be2c = sb("g2c", [P, KT]), sb("be2c", [P, KT])
        be1w = sb("be1w", [P, KT, P])
        bqc, bkc, b1c = sb("bqc", [P, KT]), sb("bkc", [P, KT]), sb("b1c", [P, FT])
        bvw, bow, bgw, b2w = (sb(n, [P, D]) for n in ("bvw", "bow", "bgw", "b2w"))
        stage = sb("stage", [P, FT * D])
        weights = {}
        for n, cols in (("q", KT * D), ("k", KT * D), ("v", KT * D), ("o", KT * D), ("g", KT * D),
                        ("1", KT * FF), ("2", FT * D)):
            weights[n] = (sb(f"w{n}_hi", [P, cols], F32R), sb(f"w{n}_lo", [P, cols], F32R))

        def tiles(n, k):
            return [w[:, :].rearrange("p (k n) -> p k n", k=k) for w in weights[n]]

        wq, wk, wv, wo, wg = (tiles(n, KT) for n in "qkvog")
        w1, w2 = tiles("1", KT), tiles("2", FT)

        x_in = sb("x_in", [P, GB, D])
        stats1, mv1, rstd1 = sb("stats1", [P, GB, 6]), sb("mv1", [P, GB, 2]), sb("rstd1", [P, GB])
        var1, half1 = sb("var1", [P, GB]), sb("half1", [P, GB], I32)
        xhat = sb("xhat", [P, GB, D])
        xT = [sb("xT_hi", [P, KT, ROWS], F32R), sb("xT_lo", [P, KT, ROWS], F32R)]
        q = [sb("q_hi", [P, KT, ROWS], F32R), sb("q_lo", [P, KT, ROWS], F32R)]
        k_full = sb("k_full", [P, KT * GB, S])
        kk = [sb("k_hi", [P, KT * GB, 2, S], F32R), sb("k_lo", [P, KT * GB, 2, S], F32R)]
        v_aug = sb("v_aug", [P, GB, H, SLOT])
        mask_in, mask_bias = sb("mask_in", [P, GB, S]), sb("mask_bias", [P, GB, S])
        scores = sb("scores", [P, CHUNKS, CH, S])
        row_max = sb("row_max", [P, CHUNKS, CH])
        carrier = sb("carrier", [P, CHUNKS])
        probs = sb("probs", [P, CPB, CH * S])
        attn_aug = sb("attn_aug", [P, GB, CPB * S])
        den_inv = sb("den_inv", [P, GB, H])
        attn = sb("attn", [P, GB, D])
        attnT = [sb("attnT_hi", [P, KT, ROWS], F32R), sb("attnT_lo", [P, KT, ROWS], F32R)]
        mem_in = sb("mem_in", [P, GB, D])
        memT = [sb("memT_hi", [P, KT, ROWS], F32R), sb("memT_lo", [P, KT, ROWS], F32R)]
        x_res = sb("x_res", [P, GB, D])
        resid = sb("resid", [P, GB, D])
        stats2, mv2, rstd2 = sb("stats2", [P, GB, 6]), sb("mv2", [P, GB, 2]), sb("rstd2", [P, GB])
        var2, half2 = sb("var2", [P, GB]), sb("half2", [P, GB], I32)
        nhalf1, nhalf2 = sb("nhalf1", [P, GB]), sb("nhalf2", [P, GB])
        newton, c1_5 = sb("newton", [P, GB]), sb("c1_5", [P, GB])
        xhat2 = sb("xhat2", [P, GB, D])
        zT = [sb("zT_hi", [P, KT, ROWS], F32R), sb("zT_lo", [P, KT, ROWS], F32R)]
        resid_b2 = sb("resid_b2", [P, GB, D])
        hid = sb("hid", [P, 2, 2, ROWS])
        hT = [sb("hT_hi", [P, FT, ROWS], F32R), sb("hT_lo", [P, FT, ROWS], F32R)]
        y = sb("y", [P, GB, D])

        score_ps = [bank("score_ps0"), bank("score_ps1")]
        turn_ps = [bank("turn_ps0"), bank("turn_ps1")]
        value_ps = bank("value_ps")
        ffn_ps = bank("ffn_ps")
        work = [bank("work_ps0"), bank("work_ps1")]
        by_tile = [w[:, :].rearrange("p (k r) -> p k r", k=KT) for w in work]
        by_seq = [w[:, :].rearrange("p (b n) -> p b n", b=GB) for w in work]

        const_loaded, stage_loaded = sem("const_loaded"), sem("stage_loaded")
        folded, split_hi, split_lo = sem("folded"), sem("split_hi"), sem("split_lo")
        shift_ready, shift_added = sem("shift_ready"), sem("shift_added")
        ones_set, be1w_set = sem("ones_set"), sem("be1w_set")
        x_loaded, mem_loaded, mask_loaded = sem("x_loaded"), sem("mem_loaded"), sem("mask_loaded")
        xres_loaded, y_stored = sem("xres_loaded"), sem("y_stored")
        ln1_stats, ln1_mean, ln1_var, ln1_half, ln1_seed, ln1_rstd, ln1_ready = (
            sem(f"ln1_{n}") for n in ("stats", "mean", "var", "half", "seed", "rstd", "ready"))
        x_turned, x_hi, x_split = sem("x_turned"), sem("x_hi"), sem("x_split")
        q_ready, q_high, q_split = sem("q_ready"), sem("q_high"), sem("q_split")
        k_ready, k_copied, k_high, k_split = sem("k_ready"), sem("k_copied"), sem("k_high"), sem("k_split")
        v_ready, values_set, bias_ready = sem("v_ready"), sem("values_set"), sem("bias_ready")
        scores_ready, scores_masked, scores_shifted = (sem(f"scores_{n}") for n in ("ready", "masked", "shifted"))
        scores_turned, probs_ready, attended = sem("scores_turned"), sem("probs_ready"), sem("attended")
        attn_copied, attn_turned, den_inverted, attn_normed = (
            sem(n) for n in ("attn_copied", "attn_turned", "den_inverted", "attn_normed"))
        attnT_ready, attnT_hi, attnT_split = sem("attnT_ready"), sem("s_attnT_hi"), sem("attnT_split")
        mem_turned, mem_hi, mem_split = sem("mem_turned"), sem("mem_hi"), sem("mem_split")
        proj_ready, xres_biased, resid_ready = sem("proj_ready"), sem("xres_biased"), sem("resid_ready")
        ln2_stats, ln2_mean, ln2_var, ln2_half, ln2_seed, ln2_rstd, ln2_ready = (
            sem(f"ln2_{n}") for n in ("stats", "mean", "var", "half", "seed", "rstd", "ready"))
        z_turned, z_hi, z_split = sem("z_turned"), sem("z_hi"), sem("z_split")
        ln1_step, ln2_step = sem("ln1_step"), sem("ln2_step")
        hid_ready, hid_relu, hid_hi, hid_split = (sem(f"s_hid_{n}") for n in ("ready", "relu", "hi", "split"))
        down_ready, resid_biased, y_summed = sem("down_ready"), sem("resid_biased"), sem("y_summed")

        def stages_before(i):
            if isinstance(i, int):
                return min(max(i + 1, 0), GROUPS), min(max(i - 1, 0), GROUPS)
            return i + 1, i - 1

        def run(eng, iteration, ahead=1):
            def peeled(i):
                iteration(i, 0 <= i + 1 < GROUPS, 0 <= i < GROUPS, 0 <= i - 1 < GROUPS,
                          0 <= i - 2 < GROUPS)
            for i in (-1, 0, 1, 2):
                peeled(i)
            with eng.Fori(3, GROUPS - ahead) as i:
                iteration(i, True, True, True, True)
            for i in range(GROUPS - ahead, GROUPS + 2):
                peeled(i)

        SETUP = (("q", wqT, KT), ("k", wkT, KT), ("v", wvT, KT), ("o", woT, KT), ("g", wgT, KT),
                 ("1", w1T, KT), ("2", w2T, FT))
        SHIFTED = "qkv1"
        CONSTS = 13

        block = ctx.enter_context(nc.Block())

        @block.sync
        def _(sp):
            sp.dma_start(stage[:, 0:KT * D].rearrange("p (k n) -> p k n", k=KT),
                         wqT.rearrange("(k p) n -> p k n", p=P)).then_inc(stage_loaded, 16)
            sp.dma_start(x_in[:], x_rows[0]).then_inc(x_loaded, 16)
            sp.dma_start(ident[:], identity).then_inc(const_loaded, 16)
            sp.dma_start(par[:], parity).then_inc(const_loaded, 16)
            for dst, src in ((g1c, g1), (be1c, be1), (g2c, g2), (be2c, be2), (bqc, bq), (bkc, bk),
                             (b1c, b1)):
                sp.dma_start(dst[:], src).then_inc(const_loaded, 16)
            for dst, src in ((bvw, bv), (bow, bo), (bgw, bg), (b2w, b2)):
                sp.dma_start(dst[:], src.rearrange("(a d) -> a d", a=1).broadcast_to([P, D])
                             ).then_inc(const_loaded, 16)
            sp.dma_start(mask_in[:], mask_rows[0]).then_inc(mask_loaded, 16)
            sp.dma_start(mem_in[:], mem_rows[0]).then_inc(mem_loaded, 16)
            sp.dma_start(x_res[:], x_rows[0]).then_inc(xres_loaded, 16)
            for n, (name, src, k) in enumerate(SETUP):
                if n == 0:
                    continue
                sp.wait_ge(split_lo, n)
                cols = k * src.shape[1]
                sp.dma_start(stage[:, 0:cols].rearrange("p (k n) -> p k n", k=k),
                             src.rearrange("(k p) n -> p k n", p=P)).then_inc(stage_loaded, 16)

            def iteration(i, front, attn_, out_, ffn):
                if ffn:
                    sp.wait_ge(y_summed, i - 1)
                    sp.dma_start(out_rows[i - 2], y[:]).then_inc(y_stored, 16)

            def loads(i):
                if not isinstance(i, int) or 0 <= i + 2 < GROUPS:
                    sp.wait_ge(ln1_ready, i + 2)
                    sp.dma_start(x_in[:], x_rows[i + 2]).then_inc(x_loaded, 16)
                if not isinstance(i, int) or 1 <= i < GROUPS:
                    sp.wait_ge(mem_turned, i)
                    sp.dma_start(mem_in[:], mem_rows[i]).then_inc(mem_loaded, 16)

            def late_loads(i):
                if not isinstance(i, int) or 1 <= i < GROUPS:
                    sp.wait_ge(resid_ready, i)
                    sp.dma_start(x_res[:], x_rows[i]).then_inc(xres_loaded, 16)
                if not isinstance(i, int) or 0 <= i + 2 < GROUPS:
                    sp.wait_ge(bias_ready, i + 2)
                    sp.dma_start(mask_in[:], mask_rows[i + 2]).then_inc(mask_loaded, 16)

            def whole(i, *flags):
                loads(i)
                late_loads(i)
                iteration(i, *flags)

            run(sp, whole, ahead=2)
            sp.wait_ge(y_stored, 16 * GROUPS)

        @block.scalar
        def _(act):
            act.wait_ge(const_loaded, 16 * CONSTS)
            for k in range(KT):
                last = act.activation(be1w[:, k, :], ident[:], ACT.Identity, bias=be1c[:, k:k + 1],
                                      scale=0.0)
            last.then_inc(be1w_set, 1)

            def split_high(src, dst, ready, count, free, freed, done):
                act.wait_ge(ready, count)
                if freed is not None:
                    act.wait_ge(free, freed)
                act.activation(dst[:], src, ACT.Copy).then_inc(done, 1)

            def iteration(i, front, attn_, out_, ffn):
                for t in range(TICKS):
                    if ffn and 1 <= t <= HJ:
                        g, n = i - 2, t - 1
                        act.wait_ge(hid_ready, HJ * g + n + 1)
                        if n >= 2 or later(g):
                            act.wait_ge(hid_split, HJ * g + n - 1)
                        for j in range(2):
                            last = act.activation(hid[:, n % 2, j, :], ffn_ps[:, j * ROWS:(j + 1) * ROWS],
                                                  ACT.Relu, bias=b1c[:, 2 * n + j:2 * n + j + 1])
                        last.then_inc(hid_relu, 1)
                    if attn_ and t in (9, 12):
                        b = 0 if t == 9 else 1
                        act.wait_ge(attended, CHUNKS * i + CPB * (b + 1))
                        if later(i):
                            act.wait_ge(attn_turned, GB * i + b - 1)
                        act.activation(attn_aug[:, b, :], value_ps[:, :], ACT.Copy).then_inc(attn_copied, 1)
                    if attn_ and 0 <= t - TURN_LAG < CHUNKS:
                        k = t - TURN_LAG
                        act.wait_ge(scores_turned, CHUNKS * i + k + 1)
                        if k >= CPB or later(i):
                            act.wait_ge(attended, CHUNKS * i + k - CPB + 1)
                        act.activation(probs[:, k % CPB, :], turn_ps[k % 2][:, :], ACT.Exp
                                       ).then_inc(probs_ready, 1)
                    if out_ and t == 2:
                        g = i - 1
                        split_high(by_tile[0], memT[0], mem_turned, g + 1, proj_ready,
                                   g if later(g) else None, mem_hi)
                    if out_ and t == 3:
                        g = i - 1
                        split_high(by_tile[1], attnT[0], attnT_ready, g + 1, proj_ready,
                                   g if later(g) else None, attnT_hi)
                    if out_ and t == 12:
                        g = i - 1
                        split_high(by_tile[0], zT[0], z_turned, g + 1, hid_ready,
                                   HJ * g if later(g) else None, z_hi)
                    if front and t == 6:
                        g = i + 1
                        split_high(by_tile[1], xT[0], x_turned, g + 1, v_ready,
                                   g if later(g) else None, x_hi)
                    if front and t == 8:
                        g = i + 1
                        act.wait_ge(q_ready, g + 1)
                        if later(g):
                            act.wait_ge(scores_ready, CHUNKS * g)
                        for k in range(KT):
                            last = act.activation(q[0][:, k, :], by_tile[0][:, k, :], ACT.Identity,
                                                  bias=bqc[:, k:k + 1])
                        last.then_inc(q_high, 1)
                    if front and t == 9:
                        g = i + 1
                        act.wait_ge(k_ready, g + 1)
                        if later(g):
                            act.wait_ge(k_split, g)
                        for k in range(KT):
                            last = act.activation(
                                k_full[:, GB * k:GB * (k + 1), :].rearrange("p b s -> p (b s)"),
                                by_tile[1][:, k, :], ACT.Identity, bias=bkc[:, k:k + 1])
                        last.then_inc(k_copied, 1)

            act.wait_ge(shift_added, 4)
            run(act, iteration)

        @block.vector
        def _(dve):
            dve.memset(c1_5[:], 1.5)
            dve.memset(v_aug[:], 1.0).then_inc(ones_set, 1)
            dve.wait_ge(const_loaded, 16 * CONSTS)

            gains = {"q": g1c, "k": g1c, "v": g1c, "1": g2c}
            n_fold = n_shift = 0
            for n, (name, src, k) in enumerate(SETUP):
                cols = src.shape[1]
                view = stage[:, 0:k * cols].rearrange("p (k n) -> p k n", k=k)
                dve.wait_ge(stage_loaded, 16 * (n + 1))
                if name in SHIFTED:
                    n_shift += 1
                    dve.wait_ge(shift_ready, n_shift)
                    if name == "q":
                        dve.scalar_tensor_tensor(out=bqc[:], in0=work[0][:, 0:KT], scalar=1.0, in1=bqc[:],
                                                 op0=ALU.mult, op1=ALU.add).then_inc(folded, 1)
                        n_fold += 1
                        dve.wait_ge(folded, n_fold)
                        dve.tensor_scalar(bqc[:], bqc[:], HD ** -0.5, None, ALU.mult).then_inc(shift_added, 1)
                    else:
                        dst, cnt = {"k": (bkc, KT), "v": (bvw, D), "1": (b1c, FT)}[name]
                        dve.tensor_tensor(dst[:], work[0][:, 0:cnt], dst[:], ALU.add).then_inc(shift_added, 1)
                    for j in range(k):
                        last = dve.tensor_scalar(view[:, j, :], view[:, j, :], gains[name][:, j:j + 1],
                                                 HD ** -0.5 if name == "q" else 1.0, ALU.mult, ALU.mult)
                    last.then_inc(folded, 1)
                    n_fold += 1
                    dve.wait_ge(folded, n_fold)
                hi, lo = weights[name]
                flat = stage[:, 0:k * cols]
                dve.tensor_copy(hi[:], flat).then_inc(split_hi, 1)
                dve.wait_ge(split_hi, n + 1)
                dve.tensor_tensor(lo[:], flat, hi[:], ALU.subtract).then_inc(split_lo, 1)
            dve.tensor_tensor(bow[:], bow[:], bgw[:], ALU.add).then_inc(shift_added, 1)

            def layer_norm_stats(g, src, stats, mv, var, nhalf, half, rstd, sems):
                stats_done, mean_done, var_done, half_done, seed_done = sems
                for b in range(GB):
                    last = dve.bn_stats(stats[:, b, :], src[:, b, :])
                last.then_inc(stats_done, 1)
                dve.wait_ge(ones_set, 1)
                dve.wait_ge(stats_done, g + 1)
                for b in range(GB):
                    last = dve.bn_aggr(mv[:, b, :], stats[:, b, :])
                last.then_inc(mean_done, 1)
                dve.wait_ge(mean_done, g + 1)
                dve.tensor_scalar(var[:], mv[:, :, 1], EPS, None, ALU.add).then_inc(var_done, 1)
                dve.tensor_scalar(nhalf[:], mv[:, :, 1], EPS, -0.5, ALU.add, ALU.mult)
                dve.wait_ge(var_done, g + 1)
                dve.tensor_scalar(half[:], var[:].bitcast(I32), 1, None, ALU.logical_shift_right
                                  ).then_inc(half_done, 1)
                dve.wait_ge(half_done, g + 1)
                dve.tensor_scalar(rstd[:].bitcast(I32), half[:], -1.0, RSQRT_SEED, ALU.mult, ALU.add
                                  ).then_inc(seed_done, 1)

            def layer_norm_apply(g, src, mv, rstd, rstd_done, dst, free, done):
                dve.wait_ge(rstd_done, g + 1)
                if later(g):
                    dve.wait_ge(free, g)
                for b in range(GB):
                    last = dve.tensor_scalar(dst[:, b, :], src[:, b, :], mv[:, b, 0:1],
                                             rstd[:, b:b + 1], ALU.subtract, ALU.mult)
                last.then_inc(done, 1)

            def split_low(src, halves, high, count, done):
                dve.wait_ge(high, count)
                dve.tensor_tensor(halves[1][:], src, halves[0][:], ALU.subtract).then_inc(done, 1)

            def iteration(i, front, attn_, out_, ffn):
                for t in range(TICKS):
                    if attn_ and t < CHUNKS:
                        b = t // CPB
                        if t == 0:
                            dve.wait_ge(bias_ready, i + 1)
                        if later(i):
                            dve.wait_ge(scores_turned, CHUNKS * (i - 1) + t + 1)
                        dve.wait_ge(scores_ready, CHUNKS * i + t + 1)
                        dve.memset(carrier[:, t:t + 1], 0.0)
                        for h in range(CH):
                            last = dve.tensor_tensor_reduce(
                                out=scores[:, t, h, :], in0=score_ps[t % 2][:, h * S:(h + 1) * S],
                                in1=mask_bias[:, b, :], scale=1.0, scalar=LOWEST, op0=ALU.add,
                                op1=ALU.max, accum_out=row_max[:, t, h:h + 1])
                        last.then_inc(scores_masked, 1)
                    if ffn and 2 <= t < HJ + 2:
                        g, n = i - 2, t - 2
                        dve.wait_ge(hid_relu, HJ * g + n + 1)
                        if n == 0 and later(g):
                            dve.wait_ge(down_ready, g)
                        dve.tensor_copy(hT[0][:, 2 * n:2 * n + 2, :], hid[:, n % 2]).then_inc(hid_hi, 1)
                    if front and t == 1:
                        dve.wait_ge(x_loaded, 16 * (i + 2))
                        layer_norm_stats(i + 1, x_in, stats1, mv1, var1, nhalf1, half1, rstd1,
                                         (ln1_stats, ln1_mean, ln1_var, ln1_half, ln1_seed))
                    if front and t == 4:
                        layer_norm_apply(i + 1, x_in, mv1, rstd1, ln1_rstd, xhat, x_turned, ln1_ready)
                    if out_ and t in (1, 2):
                        g, b = i - 1, t - 1
                        heads = work[b][:, :].rearrange("p (h e) -> p h e", h=H)
                        dve.wait_ge(attn_turned, GB * g + b + 1)
                        dve.reciprocal(den_inv[:, b, :], heads[:, :, HD]).then_inc(den_inverted, 1)
                        dve.wait_ge(den_inverted, GB * g + b + 1)
                        if later(g):
                            dve.wait_ge(attnT_ready, g)
                        dve.tensor_tensor(attn[:, b, :].rearrange("p (h e) -> p h e", h=H),
                                          heads[:, :, 0:HD],
                                          den_inv[:, b, :].unsqueeze(2).broadcast_to([P, H, HD]),
                                          ALU.mult).then_inc(attn_normed, 1)
                    if out_ and t == 3:
                        split_low(by_tile[0], memT, mem_hi, i, mem_split)
                    if out_ and t == 4:
                        split_low(by_tile[1], attnT, attnT_hi, i, attnT_split)
                    if ffn and t == 12:
                        g = i - 2
                        dve.wait_ge(down_ready, g + 1)
                        dve.wait_ge(resid_biased, g + 1)
                        if later(g):
                            dve.wait_ge(y_stored, 16 * g)
                        dve.tensor_tensor(y[:], ffn_ps[:, :].rearrange("p (b n) -> p b n", b=GB),
                                          resid_b2[:], ALU.add).then_inc(y_summed, 1)
                    if out_ and t == 7:
                        g = i - 1
                        dve.wait_ge(proj_ready, g + 1)
                        dve.wait_ge(xres_biased, g + 1)
                        if later(g):
                            dve.wait_ge(resid_biased, g)
                        dve.tensor_tensor(resid[:], by_seq[0], x_res[:], ALU.add
                                          ).then_inc(resid_ready, 1)
                    if front and t == 7:
                        split_low(by_tile[1], xT, x_hi, i + 2, x_split)
                    if out_ and t == 7:
                        dve.wait_ge(resid_ready, i)
                        layer_norm_stats(i - 1, resid, stats2, mv2, var2, nhalf2, half2, rstd2,
                                         (ln2_stats, ln2_mean, ln2_var, ln2_half, ln2_seed))
                    if out_ and t == 10:
                        layer_norm_apply(i - 1, resid, mv2, rstd2, ln2_rstd, xhat2, z_turned, ln2_ready)
                    if front and t == 9:
                        g = i + 1
                        dve.wait_ge(q_high, g + 1)
                        for k in range(KT):
                            last = dve.scalar_tensor_tensor(
                                out=q[1][:, k, :], in0=by_tile[0][:, k, :], scalar=bqc[:, k:k + 1],
                                in1=q[0][:, k, :], op0=ALU.add, op1=ALU.subtract)
                        last.then_inc(q_split, 1)
                        dve.wait_ge(mask_loaded, 16 * (g + 1))
                        dve.tensor_scalar(mask_bias[:], mask_in[:], 1.0, MASKED, ALU.subtract, ALU.mult
                                          ).then_inc(bias_ready, 1)
                    if front and t == 10:
                        g = i + 1
                        dve.wait_ge(k_copied, g + 1)
                        if later(g):
                            dve.wait_ge(scores_ready, CHUNKS * g)
                        for e in range(2):
                            last = dve.tensor_scalar(kk[0][:, :, e, :], k_full[:], par[:, e:e + 1], None,
                                                     ALU.mult)
                        last.then_inc(k_high, 1)
                        dve.wait_ge(k_high, g + 1)
                        for e in range(2):
                            last = dve.scalar_tensor_tensor(
                                out=kk[1][:, :, e, :], in0=k_full[:], scalar=par[:, e:e + 1],
                                in1=kk[0][:, :, e, :], op0=ALU.mult, op1=ALU.subtract)
                        last.then_inc(k_split, 1)
                    if out_ and t == 12:
                        split_low(by_tile[0], zT, z_hi, i, z_split)
                    if front and t == 12:
                        g = i + 1
                        dve.wait_ge(v_ready, g + 1)
                        if later(g):
                            dve.wait_ge(attended, CHUNKS * g)
                        for b in range(GB):
                            last = dve.tensor_tensor(v_aug[:, b, :, 0:HD],
                                                     by_seq[1][:, b, :].rearrange("p (h e) -> p h e", h=H),
                                                     bvw[:, :].rearrange("p (h e) -> p h e", h=H), ALU.add)
                        last.then_inc(values_set, 1)

            dve.wait_ge(shift_added, 5)
            dve.wait_ge(ones_set, 1)
            run(dve, iteration)

        @block.gpsimd
        def _(pool):
            pool.wait_ge(shift_added, 5)

            def inverse_root(g, var_half, rstd, seed_done, step_done, done):
                pool.wait_ge(seed_done, g + 1)
                steps = (4 * NEWTON_STEPS - 1) * g
                for n in range(NEWTON_STEPS):
                    if n:
                        pool.wait_ge(step_done, steps + 4 * n)
                    pool.tensor_tensor(newton[:], rstd[:], rstd[:], ALU.mult).then_inc(step_done, 1)
                    pool.wait_ge(step_done, steps + 4 * n + 1)
                    pool.tensor_tensor(newton[:], newton[:], var_half[:], ALU.mult).then_inc(step_done, 1)
                    pool.wait_ge(step_done, steps + 4 * n + 2)
                    pool.tensor_tensor(newton[:], newton[:], c1_5[:], ALU.add).then_inc(step_done, 1)
                    pool.wait_ge(step_done, steps + 4 * n + 3)
                    last = pool.tensor_tensor(rstd[:], rstd[:], newton[:], ALU.mult)
                    last.then_inc(step_done if n < NEWTON_STEPS - 1 else done, 1)

            def iteration(i, front, attn_, out_, ffn):
                for t in range(TICKS):
                    if attn_ and t < CHUNKS:
                        pool.wait_ge(scores_masked, CHUNKS * i + t + 1)
                        pool.tensor_tensor(scores[:, t], scores[:, t],
                                           row_max[:, t, :].unsqueeze(2).broadcast_to([P, CH, S]),
                                           ALU.subtract).then_inc(scores_shifted, 1)
                    if ffn and 2 <= t < HJ + 2:
                        g, n = i - 2, t - 2
                        pool.wait_ge(hid_hi, HJ * g + n + 1)
                        pool.tensor_tensor(hT[1][:, 2 * n:2 * n + 2, :], hid[:, n % 2],
                                           hT[0][:, 2 * n:2 * n + 2, :], ALU.subtract
                                           ).then_inc(hid_split, 1)
                    if front and t == 1:
                        inverse_root(i + 1, nhalf1, rstd1, ln1_seed, ln1_step, ln1_rstd)
                    if out_ and t == 8:
                        inverse_root(i - 1, nhalf2, rstd2, ln2_seed, ln2_step, ln2_rstd)
                    if out_ and t == 4:
                        pool.wait_ge(xres_loaded, 16 * i)
                        pool.tensor_tensor(x_res[:], x_res[:],
                                           bow[:, :].unsqueeze(1).broadcast_to([P, GB, D]),
                                           ALU.add).then_inc(xres_biased, 1)
                    if ffn and t == 0:
                        g = i - 2
                        pool.wait_ge(resid_ready, g + 1)
                        if later(g):
                            pool.wait_ge(y_summed, g)
                        pool.tensor_tensor(resid_b2[:], resid[:],
                                           b2w[:, :].unsqueeze(1).broadcast_to([P, GB, D]),
                                           ALU.add).then_inc(resid_biased, 1)

            run(pool, iteration)

        @block.tensor
        def _(pe):
            pe.wait_ge(const_loaded, 16 * CONSTS)
            pe.wait_ge(be1w_set, 1)
            n_shift = 0
            for n, (name, src, k) in enumerate(SETUP):
                if name not in SHIFTED:
                    continue
                cols = src.shape[1]
                view = stage[:, 0:k * cols].rearrange("p (k n) -> p k n", k=k)
                pe.wait_ge(stage_loaded, 16 * (n + 1))
                if n_shift:
                    pe.wait_ge(shift_added, n_shift)
                shift = be2c if name == "1" else be1c
                if name == "v":
                    for j in range(k):
                        last = pe.matmul(work[0][:, 0:D], be1w[:, j, :], view[:, j, :], start=(j == 0),
                                         stop=(j == k - 1))
                else:
                    for m in range(cols // P):
                        for j in range(k):
                            last = pe.matmul(work[0][:, m:m + 1], view[:, j, m * P:(m + 1) * P],
                                             shift[:, j:j + 1], start=(j == 0), stop=(j == k - 1))
                last.then_inc(shift_ready, 1)
                n_shift += 1

            def product(dst, pairs, start=True, stop=True, **more):
                n = len(pairs)
                for j, (lhs, rhs) in enumerate(pairs):
                    pe.matmul(dst, lhs[1], rhs[0], start=start and j == 0, stop=False, **more)
                    pe.matmul(dst, lhs[0], rhs[1], start=False, stop=False, **more)
                    last = pe.matmul(dst, lhs[0], rhs[0], start=False, stop=stop and j == n - 1, **more)
                return last

            def cut(pair, *at):
                return pair[0][at], pair[1][at]

            ALL = slice(None)

            def seq(b):
                return slice(b * S, (b + 1) * S)

            def turn(dst, src):
                for k in range(KT):
                    for b in range(GB):
                        last = pe.transpose(dst[:, k, seq(b)], src[:, b, k * P:(k + 1) * P], ident[:])
                return last

            def iteration(i, front, attn_, out_, ffn):
                fronts, outs = stages_before(i)
                for t in range(TICKS):
                    if attn_ and t < CHUNKS:
                        b, c = divmod(t, CPB)
                        if t == 0:
                            pe.wait_ge(q_split, i + 1)
                            pe.wait_ge(k_split, i + 1)
                        if t >= 2 or later(i):
                            pe.wait_ge(scores_masked, CHUNKS * i + t - 1)
                        rows = slice(32 * c, 32 * c + 32)
                        for k in range(KT):
                            dst = score_ps[t % 2][:, k * 2 * S:(k + 1) * 2 * S]
                            keys = [h[rows, GB * k + b].rearrange("p e s -> p (e s)") for h in kk]
                            last = product(dst, [(cut(q, rows, k, seq(b)), keys)])
                        last.then_inc(scores_ready, 1)
                    if attn_ and 0 <= t - TURN_LAG < CHUNKS:
                        k = t - TURN_LAG
                        pe.wait_ge(scores_shifted, CHUNKS * i + k + 1)
                        if k >= 2 or later(i):
                            pe.wait_ge(probs_ready, CHUNKS * i + k - 1)
                        for h in range(CH):
                            last = pe.transpose(turn_ps[k % 2][:, h * S:(h + 1) * S], scores[:, k, h, :],
                                                ident[:])
                        last.then_inc(scores_turned, 1)
                    if out_ and t in (0, 1):
                        g, b = i - 1, t
                        pe.wait_ge(attn_copied, GB * g + b + 1)
                        if b == 0 and later(outs):
                            pe.wait_ge(z_split, outs)
                        elif b == 0:
                            pe.wait_ge(q_split, fronts)
                        else:
                            pe.wait_ge(values_set, fronts)
                            if isinstance(i, int) and outs > 0:
                                pe.wait_ge(attnT_split, outs)
                        for c in range(CPB):
                            last = pe.transpose(work[b][:, c * S:(c + 1) * S],
                                                attn_aug[:, b, c * S:(c + 1) * S], ident[:])
                        last.then_inc(attn_turned, 1)
                    if out_ and t == 2:
                        pe.wait_ge(mem_loaded, 16 * i)
                        pe.wait_ge(attn_normed, GB * i - 1)
                        turn(by_tile[0], mem_in).then_inc(mem_turned, 1)
                    if out_ and t == 3:
                        pe.wait_ge(attn_normed, GB * i)
                        turn(by_tile[1], attn).then_inc(attnT_ready, 1)
                    if ffn and 1 <= t <= HJ:
                        g, n = i - 2, t - 1
                        if n == 0:
                            pe.wait_ge(z_split, g + 1)
                            if later(g):
                                pe.wait_ge(y_summed, g)
                        else:
                            pe.wait_ge(hid_relu, HJ * g + n)
                        for j in range(2):
                            f = 2 * n + j
                            last = product(ffn_ps[:, j * ROWS:(j + 1) * ROWS],
                                           [(cut(w1, ALL, k, slice(f * P, (f + 1) * P)), cut(zT, ALL, k))
                                            for k in range(KT)])
                        last.then_inc(hid_ready, 1)
                    if out_ and t in (5, 6):
                        b = t - 5
                        if b == 0:
                            pe.wait_ge(attnT_split, i)
                            pe.wait_ge(mem_split, i)
                        last = product(by_seq[0][:, b, :],
                                       [(cut(attnT, ALL, k, seq(b)), cut(wo, ALL, k)) for k in range(KT)]
                                       + [(cut(memT, ALL, k, seq(b)), cut(wg, ALL, k)) for k in range(KT)])
                        if b == GB - 1:
                            last.then_inc(proj_ready, 1)
                    if front and t == 6:
                        pe.wait_ge(ln1_ready, i + 2)
                        if out_:
                            pe.wait_ge(attnT_split, i)
                        elif later(i + 1):
                            pe.wait_ge(values_set, i + 1)
                        turn(by_tile[1], xhat).then_inc(x_turned, 1)
                    if front and t in (8, 9):
                        which = t - 8
                        if which == 0:
                            pe.wait_ge(x_split, i + 2)
                            if out_:
                                pe.wait_ge(resid_ready, i)
                            elif later(i + 1):
                                pe.wait_ge(q_split, i + 1)
                        for m in range(KT):
                            last = product(by_tile[which][:, m, :],
                                           [(cut((wq, wk)[which], ALL, k, slice(m * P, (m + 1) * P)),
                                             cut(xT, ALL, k)) for k in range(KT)])
                        last.then_inc((q_ready, k_ready)[which], 1)
                    if ffn and t in DOWN_TICKS:
                        g, part = i - 2, DOWN_TICKS.index(t)
                        if part == 0:
                            pe.wait_ge(hid_relu, HJ * g + HJ)
                        pe.wait_ge(hid_split, HJ * g + part + 1)
                        for f in range(2 * part, 2 * part + 2):
                            for b in range(GB):
                                last = product(ffn_ps[:, b * D:(b + 1) * D],
                                               [(cut(hT, ALL, f, seq(b)), cut(w2, ALL, f))],
                                               start=(f == 0 and b == 0), stop=(f == FT - 1),
                                               skip_group_check=True)
                        if part == HJ - 1:
                            last.then_inc(down_ready, 1)
                    if attn_ and t >= VALUE_LAG:
                        k = t - VALUE_LAG
                        b, c = divmod(k, CPB)
                        pe.wait_ge(probs_ready, CHUNKS * i + k + 1)
                        if k == 0:
                            pe.wait_ge(values_set, i + 1)
                        if c == 0 and (b or later(i)):
                            pe.wait_ge(attn_copied, GB * i + b)
                        for h in range(CH):
                            last = pe.matmul(value_ps[SLOT * h:SLOT * (h + 1), c * S:(c + 1) * S],
                                             v_aug[:, b, head_of(c, h), :], probs[:, c, h * S:(h + 1) * S],
                                             start=True, stop=True)
                        last.then_inc(attended, 1)
                    if out_ and t == 12:
                        pe.wait_ge(ln2_ready, i)
                        if front:
                            pe.wait_ge(q_split, i + 2)
                        turn(by_tile[0], xhat2).then_inc(z_turned, 1)
                    if front and t == 12:
                        pe.wait_ge(k_copied, i + 2)
                        for b in range(GB):
                            last = product(by_seq[1][:, b, :],
                                           [(cut(xT, ALL, k, seq(b)), cut(wv, ALL, k)) for k in range(KT)])
                        last.then_inc(v_ready, 1)

            pe.wait_ge(split_lo, len(SETUP))
            run(pe, iteration)


def kernel(**inputs):
    import numpy as np
    import concourse.bacc as bacc
    from concourse.bass_utils import run_bass_kernel_spmd

    nc = bacc.Bacc("TRN2", target_bir_lowering=False, num_devices=1)
    arrays, args = {}, []

    def give(name, a):
        arrays[name] = np.ascontiguousarray(a)
        args.append(nc.dram_tensor(name, arrays[name].shape, mybir.dt.from_np(arrays[name].dtype),
                                   kind="ExternalInput").ap())

    give("x_dram", inputs["x"])
    give("memory_dram", inputs["ctx_1024"])
    give("mask_dram", inputs["mask_BxSxS2_fk0"])
    order = [16 * head_of(c, h) + e for c in range(4) for h in range(4) for e in range(16)]
    for n in ("Wq", "Wk", "Wv", "Wo", "Wg", "W1", "W2"):
        wT = np.asarray(inputs[f"L0_xattn_{n}"]).T
        give(f"{n}T_dram", wT[order] if n == "Wo" else wT)
    for n in ("bq", "bk", "bv", "bo", "bg", "b1", "b2", "g1", "be1", "g2", "be2"):
        a = np.asarray(inputs[f"L0_xattn_{n}"])
        give(f"{n}_dram", a if n in ("bv", "bo", "bg", "b2") else a.reshape(-1, P).T)
    give("identity_dram", np.eye(P, dtype=np.float32))
    even = (np.arange(P) // 16) % 2 == 0
    give("parity_dram", np.stack([even, ~even], axis=1).astype(np.float32))
    shape = tuple(inputs["x"].shape)
    args.append(nc.dram_tensor("out_dram", shape, F32, kind="ExternalOutput").ap())
    xattn_block(nc, *args)
    r = run_bass_kernel_spmd(nc, [arrays], core_ids=[0])
    return r.results[0]["out_dram"]
```

```python
from contextlib import ExitStack

import concourse.bass as bass
from concourse import mybir

ALU = mybir.AluOpType
ACT = mybir.ActivationFunctionType
F32 = mybir.dt.float32
F32R = mybir.dt.float32r
I32 = mybir.dt.int32

P = 128
EPS = 1e-5
MASKED = 1e9
LOWEST = -3.0e38
RSQRT_SEED = float(0x5F3759DF)
NEWTON_STEPS = 3

TICKS = 13
TURN_LAG = 3
SCORE_TICKS = {2: 3, 3: 4, 5: 5, 6: 6, 7: 7}
UP_TICKS = (0, 2, 4, 7)
HIDDEN_TICKS = (1, 3, 5, 8)
DOWN_TICKS = (9, 10, 11, 12)
VALUE_TICKS = (6, 8, 10, 12)


VECTORS = (("g1", 2), ("be1", 2), ("g2", 2), ("be2", 2), ("bq", 2), ("bk", 2), ("b1", 8), ("even_odd", 2))


def later(g):
    return not (isinstance(g, int) and g == 0)


def is_at(i, n):
    return isinstance(i, int) and i == n


def head_of(c, h):
    return 8 * (h // 2) + 2 * c + h % 2


def xattn_block(nc, x, memory, mask, wqT, wkT, wvT, woT, wgT, w1T, w2T,
                vectors, rows, identity, out):
    B, S, D = x.shape
    FF = w1T.shape[1]
    H = 16
    HD = D // H
    GB = 2
    GROUPS = B // GB
    ROWS = GB * S
    KT = D // P
    FT = FF // P
    CH = 4
    CPB = H // CH
    CHUNKS = GB * CPB
    HJ = FT // 2
    SLOT = 32
    assert S == P and D == 2 * P and CHUNKS == 8 and HJ == 4

    x_rows = x.rearrange("(g b) s d -> g s b d", b=GB)
    mem_cols = memory.rearrange("(k p) (g r) -> g p k r", p=P, r=ROWS)
    mask_rows = mask.rearrange("(g b) s t -> g s b t", b=GB)
    out_rows = out.rearrange("(g b) s d -> g s b d", b=GB)

    with ExitStack() as ctx:
        def sb(name, shape, dt=F32):
            return ctx.enter_context(nc.sbuf_tensor(name, shape, dt))

        def bank(name):
            return ctx.enter_context(nc.psum_tensor(name, [P, 512], F32))

        def sem(name):
            return ctx.enter_context(nc.semaphore(name))

        ident = sb("ident", [P, P])
        vector_cols, at = {}, 0
        vec = sb("vec", [P, sum(n for _, n in VECTORS)])
        for name, n in VECTORS:
            vector_cols[name] = vec[:, at:at + n]
            at += n
        g1c, be1c, g2c, be2c, bqc, bkc, b1c, par = (vector_cols[name] for name, _ in VECTORS)
        row = sb("row", [P, 4, D])
        bvw, bow, bgw, b2w = (row[:, n, :] for n in range(4))
        be1w = sb("be1w", [P, KT, P])
        weights = {}
        for n, cols in (("q", KT * D), ("k", KT * D), ("v", KT * D), ("o", KT * D), ("g", KT * D),
                        ("1", KT * FF), ("2", FT * D)):
            weights[n] = (sb(f"w{n}_hi", [P, cols], F32R), sb(f"w{n}_lo", [P, cols], F32R))

        def tiles(n, k):
            return [w[:, :].rearrange("p (k n) -> p k n", k=k) for w in weights[n]]

        wq, wk, wv, wo, wg = (tiles(n, KT) for n in "qkvog")
        w1, w2 = tiles("1", KT), tiles("2", FT)

        x_in = sb("x_in", [P, GB, D])
        stats1, mv1 = sb("stats1", [P, GB, 6]), sb("mv1", [P, GB, 2])
        var1, half1 = sb("var1", [P, GB]), sb("half1", [P, GB], I32)
        xhat = sb("xhat", [P, GB, D])
        xT = [sb("xT_hi", [P, KT, ROWS], F32R), sb("xT_lo", [P, KT, ROWS], F32R)]
        q = [sb("q_hi", [P, KT, ROWS], F32R), sb("q_lo", [P, KT, ROWS], F32R)]
        k_full = sb("k_full", [P, KT * GB, S])
        kk = [sb("k_hi", [P, KT * GB, 2, S], F32R), sb("k_lo", [P, KT * GB, 2, S], F32R)]
        q_stack = sb("q_stack", [P, CPB, KT, ROWS], F32R)
        k_stack = sb("k_stack", [P, CPB, KT * GB, 2, S], F32R)
        v_aug = sb("v_aug", [P, GB, H, SLOT])
        mask_in, mask_bias = sb("mask_in", [P, GB, S]), sb("mask_bias", [P, GB, S])
        scores = sb("scores", [P, CHUNKS, CH, S])
        row_max = sb("row_max", [P, CHUNKS, CH])
        carrier = sb("carrier", [P, CHUNKS])
        probs = sb("probs", [P, CPB, CH * S])
        attn_aug = sb("attn_aug", [P, GB, CPB * S])
        den_inv = sb("den_inv", [P, GB, H])
        attn = sb("attn", [P, GB, D])
        attnT = [sb("attnT_hi", [P, KT, ROWS], F32R), sb("attnT_lo", [P, KT, ROWS], F32R)]
        mem_in = sb("mem_in", [P, KT, ROWS])
        memT = [sb("memT_hi", [P, KT, ROWS], F32R), sb("memT_lo", [P, KT, ROWS], F32R)]
        x_res = sb("x_res", [P, GB, D])
        resid = sb("resid", [P, GB, D])
        stats2, mv2 = sb("stats2", [P, GB, 6]), sb("mv2", [P, GB, 2])
        var2, half2 = sb("var2", [P, GB]), sb("half2", [P, GB], I32)
        rstds, nhalfs = sb("rstds", [P, 2, GB]), sb("nhalfs", [P, 2, GB])
        newton, c1_5 = sb("newton", [P, 2, GB]), sb("c1_5", [P, 2, GB])
        rstd1, rstd2 = rstds[:, 0, :], rstds[:, 1, :]
        nhalf1, nhalf2 = nhalfs[:, 0, :], nhalfs[:, 1, :]
        xhat2 = sb("xhat2", [P, GB, D])
        zT = [sb("zT_hi", [P, KT, ROWS], F32R), sb("zT_lo", [P, KT, ROWS], F32R)]
        resid_b2 = sb("resid_b2", [P, GB, D])
        hid = sb("hid", [P, 2, 2, ROWS])
        hT = [sb("hT_hi", [P, FT, ROWS], F32R), sb("hT_lo", [P, FT, ROWS], F32R)]
        y = sb("y", [P, GB, D])

        score_ps = [bank("score_ps0"), bank("score_ps1")]
        turn_ps = [bank("turn_ps0"), bank("turn_ps1")]
        value_ps = bank("value_ps")
        ffn_ps = bank("ffn_ps")
        work = [bank("work_ps0"), bank("work_ps1")]
        by_tile = [w[:, :].rearrange("p (k r) -> p k r", k=KT) for w in work]
        by_seq = [w[:, :].rearrange("p (b n) -> p b n", b=GB) for w in work]

        vec_loaded, row_loaded, ident_loaded = sem("vec_loaded"), sem("row_loaded"), sem("ident_loaded")
        weight_loaded = {n: sem(f"w{n}_loaded") for n in "qkvog12"}
        folded, up_folded = sem("folded"), sem("up_folded")
        split_hi, weights_hi, split_lo = sem("split_hi"), sem("weights_hi"), sem("split_lo")
        rows_summed, c1_5_set = sem("rows_summed"), sem("c1_5_set")
        shift_ready, shift_added = sem("shift_ready"), sem("shift_added")
        ones_set, be1w_set = sem("ones_set"), sem("be1w_set")
        x_loaded, mem_loaded, mask_loaded = sem("x_loaded"), sem("mem_loaded"), sem("mask_loaded")
        xres_loaded, y_stored = sem("xres_loaded"), sem("y_stored")
        ln1_stats, ln1_mean, ln1_var, ln1_half, ln1_seed, ln1_ready = (
            sem(f"ln1_{n}") for n in ("stats", "mean", "var", "half", "seed", "ready"))
        x_turned, x_hi, x_split = sem("x_turned"), sem("x_hi"), sem("x_split")
        q_ready, q_high, q_split = sem("q_ready"), sem("q_high"), sem("q_split")
        k_ready, k_copied, k_high, k_split = sem("k_ready"), sem("k_copied"), sem("k_high"), sem("k_split")
        zeros_set = sem("zeros_set")
        q_stacked, k_stacked = sem("q_stacked"), [sem(f"k_stacked{r}") for r in range(CPB)]
        v_ready, values_set, bias_ready = sem("v_ready"), sem("values_set"), sem("bias_ready")
        scores_ready, scores_masked, scores_shifted = (sem(f"scores_{n}") for n in ("ready", "masked", "shifted"))
        scores_turned, probs_ready, attended = sem("scores_turned"), sem("probs_ready"), sem("attended")
        attn_copied, attn_turned, den_inverted, attn_normed = (
            sem(n) for n in ("attn_copied", "attn_turned", "den_inverted", "attn_normed"))
        attnT_ready, attnT_hi, attnT_split = sem("attnT_ready"), sem("s_attnT_hi"), sem("attnT_split")
        mem_hi, mem_split = sem("mem_hi"), sem("mem_split")
        proj_ready, xres_biased, resid_ready = sem("proj_ready"), sem("xres_biased"), sem("resid_ready")
        ln2_stats, ln2_mean, ln2_var, ln2_half, ln2_seed, ln2_ready = (
            sem(f"ln2_{n}") for n in ("stats", "mean", "var", "half", "seed", "ready"))
        z_turned, z_hi, z_split = sem("z_turned"), sem("z_hi"), sem("z_split")
        ln_step, ln_rstd = sem("ln_step"), sem("ln_rstd")
        hid_ready, hid_relu, hid_hi, hid_split = (sem(f"s_hid_{n}") for n in ("ready", "relu", "hi", "split"))
        down_ready, resid_biased, y_summed = sem("down_ready"), sem("resid_biased"), sem("y_summed")

        def stages_before(i):
            if isinstance(i, int):
                return min(max(i + 1, 0), GROUPS), min(max(i - 1, 0), GROUPS)
            return i + 1, i - 1

        def run(eng, iteration, ahead=2, after_first=None, after_second=None):
            def peeled(i):
                iteration(i, *(0 <= g < GROUPS for g in (i + 2, i + 1, i, i - 1, i - 2)))
            for i in range(-2, 3):
                peeled(i)
                if i == -2 and after_first is not None:
                    after_first()
                if i == -1 and after_second is not None:
                    after_second()
            with eng.Fori(3, GROUPS - ahead) as i:
                iteration(i, True, True, True, True, True)
            for i in range(GROUPS - ahead, GROUPS + 2):
                peeled(i)

        SETUP = {"q": (wqT, KT), "k": (wkT, KT), "v": (wvT, KT), "o": (woT, KT), "g": (wgT, KT),
                 "1": (w1T, KT), "2": (w2T, FT)}
        SPLIT_AT = {n: j + 1 for j, n in enumerate(SETUP)}
        SHIFTED = "qkv1"
        SHIFTS_AT = {"q": ffn_ps[:, 0:KT], "k": score_ps[0][:, 0:KT], "v": score_ps[1][:, 0:D],
                     "1": value_ps[:, 0:FT]}
        TERMS = 3

        def raw(name):
            if name == "2":
                return probs[:].rearrange("p c n -> p (c n)")
            if name == "g":
                return y[:].rearrange("p b n -> p (b n)")
            at, n = {"q": (0, 1), "k": (1, 1), "v": (2, 1), "o": (3, 1), "1": (4, 4)}[name]
            return scores[:, at:at + n].rearrange("p t h s -> p (t h s)")

        block = ctx.enter_context(nc.Block())

        @block.sync
        def _(sp):
            def load_weight(name):
                src, k = SETUP[name]
                sp.dma_start(raw(name).rearrange("p (k n) -> p k n", k=k),
                             src.rearrange("(k p) n -> p k n", p=P)).then_inc(weight_loaded[name], 16)

            sp.dma_start(x_in[:], x_rows[0]).then_inc(x_loaded, 16)
            sp.dma_start(vec[:], vectors).then_inc(vec_loaded, 16)
            load_weight("q")
            sp.dma_start(ident[:], identity).then_inc(ident_loaded, 16)
            load_weight("k")
            load_weight("v")
            sp.dma_start(row[:].rearrange("p n d -> p (n d)"),
                         rows.rearrange("(a d) -> a d", a=1).broadcast_to([P, 4 * D])
                         ).then_inc(row_loaded, 16)
            sp.dma_start(mask_in[:], mask_rows[0]).then_inc(mask_loaded, 16)
            load_weight("o")
            load_weight("g")
            sp.dma_start(mem_in[:], mem_cols[0]).then_inc(mem_loaded, 16)
            sp.dma_start(x_res[:], x_rows[0]).then_inc(xres_loaded, 16)
            load_weight("1")
            load_weight("2")

            def known(i, low, high):
                return not isinstance(i, int) or low <= i < high

            def iteration(i, norm, front, attn_, out_, ffn):
                if front:
                    sp.wait_ge(q_split, i + 2)
                    for r in range(CPB):
                        if later(i + 1):
                            sp.wait_ge(scores_ready, CHUNKS * i + CPB + r + 1)
                        for j, high_low in enumerate((1, 0, 0)):
                            sp.dma_start(q_stack[32 * j:32 * j + 32, r].bitcast(F32),
                                         q[high_low][32 * r:32 * r + 32].bitcast(F32)
                                         ).then_inc(q_stacked, 16)
                    sp.wait_ge(k_split, i + 2)
                    for r in range(CPB):
                        for j, high_low in enumerate((0, 1, 0)):
                            sp.dma_start(k_stack[32 * j:32 * j + 32, r].bitcast(F32),
                                         kk[high_low][32 * r:32 * r + 32].bitcast(F32)
                                         ).then_inc(k_stacked[r], 16)
                if known(i, 1, GROUPS):
                    sp.wait_ge(resid_ready, i)
                    sp.dma_start(x_res[:], x_rows[i]).then_inc(xres_loaded, 16)
                if known(i, -1, GROUPS - 2):
                    sp.wait_ge(bias_ready, i + 2)
                    sp.dma_start(mask_in[:], mask_rows[i + 2]).then_inc(mask_loaded, 16)
                if known(i, 0, GROUPS - 1):
                    sp.wait_ge(mem_split, i + 1)
                    sp.dma_start(mem_in[:], mem_cols[i + 1]).then_inc(mem_loaded, 16)
                if known(i, -2, GROUPS - 3):
                    sp.wait_ge(ln1_ready, i + 3)
                    sp.dma_start(x_in[:], x_rows[i + 3]).then_inc(x_loaded, 16)
                if ffn:
                    sp.wait_ge(y_summed, i - 1)
                    sp.dma_start(out_rows[i - 2], y[:]).then_inc(y_stored, 16)

            run(sp, iteration, ahead=3)
            sp.wait_ge(y_stored, 16 * GROUPS)

        @block.scalar
        def _(act):
            act.wait_ge(vec_loaded, 16)
            act.wait_ge(ident_loaded, 16)
            for k in range(KT):
                last = act.activation(be1w[:, k, :], ident[:], ACT.Identity, bias=be1c[:, k:k + 1],
                                      scale=0.0)
            last.then_inc(be1w_set, 1)

            def split_high(src, dst, ready, count, free, freed, done):
                act.wait_ge(ready, count)
                if freed is not None:
                    act.wait_ge(free, freed)
                act.activation(dst[:], src, ACT.Copy).then_inc(done, 1)

            def iteration(i, norm, front, attn_, out_, ffn):
                for t in range(TICKS):
                    if is_at(i, 2) and t == 0:
                        act.wait_ge(shift_added, 4)
                    if front and t == 0:
                        g = i + 1
                        split_high(by_tile[1], xT[0], x_turned, g + 1, v_ready,
                                   g if later(g) else None, x_hi)
                    if ffn and t in UP_TICKS:
                        g, n = i - 2, UP_TICKS.index(t)
                        act.wait_ge(hid_ready, HJ * g + n + 1)
                        if n >= 2 or later(g):
                            act.wait_ge(hid_split, HJ * g + n - 1)
                        for j in range(2):
                            last = act.activation(hid[:, n % 2, j, :], ffn_ps[:, j * ROWS:(j + 1) * ROWS],
                                                  ACT.Relu, bias=b1c[:, 2 * n + j:2 * n + j + 1])
                        last.then_inc(hid_relu, 1)
                    if out_ and t == 2:
                        g = i - 1
                        split_high(by_tile[1], attnT[0], attnT_ready, g + 1, proj_ready,
                                   g if later(g) else None, attnT_hi)
                    if attn_ and t in (9, 12):
                        b = 0 if t == 9 else 1
                        act.wait_ge(attended, CHUNKS * i + CPB * (b + 1))
                        if later(i):
                            act.wait_ge(attn_turned, GB * i + b - 1)
                        act.activation(attn_aug[:, b, :], value_ps[:, :], ACT.Copy).then_inc(attn_copied, 1)
                    if attn_ and 0 <= t - TURN_LAG < CHUNKS:
                        k = t - TURN_LAG
                        act.wait_ge(scores_turned, CHUNKS * i + k + 1)
                        if k >= CPB or later(i):
                            act.wait_ge(attended, CHUNKS * i + k - CPB + 1)
                        act.activation(probs[:, k % CPB, :], turn_ps[k % 2][:, :], ACT.Exp
                                       ).then_inc(probs_ready, 1)
                    if out_ and t == 11:
                        g = i - 1
                        split_high(by_tile[1], zT[0], z_turned, g + 1, hid_ready,
                                   HJ * g if later(g) else None, z_hi)
                    if front and t == 1:
                        g = i + 1
                        if not later(g):
                            act.wait_ge(shift_added, 2)
                        act.wait_ge(q_ready, g + 1)
                        if later(g):
                            act.wait_ge(q_stacked, 16 * TERMS * CPB * g)
                        for k in range(KT):
                            last = act.activation(q[0][:, k, :], by_tile[0][:, k, :], ACT.Identity,
                                                  bias=bqc[:, k:k + 1])
                        last.then_inc(q_high, 1)
                    if front and t == 3:
                        g = i + 1
                        act.wait_ge(k_ready, g + 1)
                        if later(g):
                            act.wait_ge(k_split, g)
                        for k in range(KT):
                            last = act.activation(
                                k_full[:, GB * k:GB * (k + 1), :].rearrange("p b s -> p (b s)"),
                                by_tile[0][:, k, :], ACT.Identity, bias=bkc[:, k:k + 1])
                        last.then_inc(k_copied, 1)

            def high_parts():
                for n, name in enumerate("og12"):
                    act.wait_ge(weight_loaded[name], 16)
                    if name == "1":
                        act.wait_ge(shift_ready, len(SHIFTED))
                        w = raw("1").rearrange("p (k n) -> p k n", k=KT)
                        for k in range(KT):
                            last = act.activation(w[:, k, :], w[:, k, :], ACT.Copy, scale=g2c[:, k:k + 1])
                        last.then_inc(up_folded, 1)
                        act.wait_ge(up_folded, 1)
                    act.activation(weights[name][0][:], raw(name), ACT.Copy).then_inc(weights_hi, 1)

            run(act, iteration, after_second=high_parts)

        @block.vector
        def _(dve):
            dve.memset(rstds[:], 1.0)
            dve.memset(nhalfs[:], -0.5)
            dve.memset(v_aug[:], 1.0).then_inc(ones_set, 1)
            dve.wait_ge(vec_loaded, 16)
            dve.wait_ge(ones_set, 1)

            def add_shift(name):
                dst = {"q": bqc, "k": bkc, "v": bvw, "1": b1c}[name]
                dve.wait_ge(shift_ready, SHIFTED.index(name) + 1)
                if name == "v":
                    dve.wait_ge(row_loaded, 16)
                add = dve.tensor_tensor(dst, SHIFTS_AT[name], dst, ALU.add)
                if name != "q":
                    add.then_inc(shift_added, 1)
                    return
                add.then_inc(folded, 1)
                dve.wait_ge(folded, 1)
                dve.tensor_scalar(bqc, bqc, HD ** -0.5, None, ALU.mult).then_inc(shift_added, 1)

            def low_part(name):
                dve.tensor_tensor(weights[name][1][:], raw(name), weights[name][0][:], ALU.subtract
                                  ).then_inc(split_lo, 1)

            def fold_and_split(name):
                dve.wait_ge(weight_loaded[name], 16)
                add_shift(name)
                view = raw(name).rearrange("p (k n) -> p k n", k=KT)
                for j in range(KT):
                    last = dve.tensor_scalar(view[:, j, :], view[:, j, :], g1c[:, j:j + 1],
                                             HD ** -0.5 if name == "q" else 1.0, ALU.mult, ALU.mult)
                last.then_inc(folded, 1)
                n = SHIFTED.index(name)
                dve.wait_ge(folded, n + 2)
                dve.tensor_copy(weights[name][0][:], raw(name)).then_inc(split_hi, 1)
                dve.wait_ge(split_hi, n + 1)
                low_part(name)

            def keys_and_values():
                fold_and_split("k")
                fold_and_split("v")

            def low_parts():
                dve.tensor_tensor(bow, bow, bgw, ALU.add).then_inc(rows_summed, 1)
                add_shift("1")
                for n, name in enumerate("og12"):
                    dve.wait_ge(weights_hi, n + 1)
                    low_part(name)

            def layer_norm_stats(g, src, stats, mv, var, nhalf, half, rstd, sems):
                stats_done, mean_done, var_done, half_done, seed_done = sems
                for b in range(GB):
                    last = dve.bn_stats(stats[:, b, :], src[:, b, :])
                last.then_inc(stats_done, 1)
                dve.wait_ge(ones_set, 1)
                dve.wait_ge(stats_done, g + 1)
                for b in range(GB):
                    last = dve.bn_aggr(mv[:, b, :], stats[:, b, :])
                last.then_inc(mean_done, 1)
                dve.wait_ge(mean_done, g + 1)
                dve.tensor_scalar(var[:], mv[:, :, 1], EPS, None, ALU.add).then_inc(var_done, 1)
                dve.tensor_scalar(nhalf, mv[:, :, 1], EPS, -0.5, ALU.add, ALU.mult)
                dve.wait_ge(var_done, g + 1)
                dve.tensor_scalar(half[:], var[:].bitcast(I32), 1, None, ALU.logical_shift_right
                                  ).then_inc(half_done, 1)
                dve.wait_ge(half_done, g + 1)
                dve.tensor_scalar(rstd.bitcast(I32), half[:], -1.0, RSQRT_SEED, ALU.mult, ALU.add
                                  ).then_inc(seed_done, 1)

            def layer_norm_apply(g, rooted, src, mv, rstd, dst, free, done):
                dve.wait_ge(ln_rstd, rooted)
                if later(g):
                    dve.wait_ge(free, g)
                for b in range(GB):
                    last = dve.tensor_scalar(dst[:, b, :], src[:, b, :], mv[:, b, 0:1],
                                             rstd[:, b:b + 1], ALU.subtract, ALU.mult)
                last.then_inc(done, 1)

            def split_low(src, halves, high, count, done):
                dve.wait_ge(high, count)
                dve.tensor_tensor(halves[1][:], src, halves[0][:], ALU.subtract).then_inc(done, 1)

            def iteration(i, norm, front, attn_, out_, ffn):
                for t in range(TICKS):
                    if attn_ and t < CHUNKS:
                        b = t // CPB
                        if t == 0:
                            dve.wait_ge(bias_ready, i + 1)
                        if later(i):
                            dve.wait_ge(scores_turned, CHUNKS * (i - 1) + t + 1)
                        dve.wait_ge(scores_ready, CHUNKS * i + t + 1)
                        dve.memset(carrier[:, t:t + 1], 0.0)
                        for h in range(CH):
                            last = dve.tensor_tensor_reduce(
                                out=scores[:, t, h, :], in0=score_ps[t % 2][:, h * S:(h + 1) * S],
                                in1=mask_bias[:, b, :], scale=1.0, scalar=LOWEST, op0=ALU.add,
                                op1=ALU.max, accum_out=row_max[:, t, h:h + 1])
                        last.then_inc(scores_masked, 1)
                    if front and t == 0:
                        split_low(by_tile[1], xT, x_hi, i + 2, x_split)
                    if out_ and t in (0, 1):
                        g, b = i - 1, t
                        heads = work[b][:, :].rearrange("p (h e) -> p h e", h=H)
                        dve.wait_ge(attn_turned, GB * g + b + 1)
                        dve.reciprocal(den_inv[:, b, :], heads[:, :, HD]).then_inc(den_inverted, 1)
                        dve.wait_ge(den_inverted, GB * g + b + 1)
                        if later(g):
                            dve.wait_ge(attnT_ready, g)
                        dve.tensor_tensor(attn[:, b, :].rearrange("p (h e) -> p h e", h=H),
                                          heads[:, :, 0:HD],
                                          den_inv[:, b, :].unsqueeze(2).broadcast_to([P, H, HD]),
                                          ALU.mult).then_inc(attn_normed, 1)
                    if out_ and t == 3:
                        split_low(by_tile[1], attnT, attnT_hi, i, attnT_split)
                    if ffn and t in HIDDEN_TICKS:
                        g, n = i - 2, HIDDEN_TICKS.index(t)
                        dve.wait_ge(hid_relu, HJ * g + n + 1)
                        if n == 0 and later(g):
                            dve.wait_ge(down_ready, g)
                        dve.tensor_copy(hT[0][:, 2 * n:2 * n + 2, :], hid[:, n % 2]).then_inc(hid_hi, 1)
                    if is_at(i, -1) and t == 2:
                        dve.wait_ge(shift_added, 3)
                    if front and t == 2:
                        g = i + 1
                        dve.wait_ge(q_high, g + 1)
                        for k in range(KT):
                            last = dve.scalar_tensor_tensor(
                                out=q[1][:, k, :], in0=by_tile[0][:, k, :], scalar=bqc[:, k:k + 1],
                                in1=q[0][:, k, :], op0=ALU.add, op1=ALU.subtract)
                        last.then_inc(q_split, 1)
                    if front and t == 4:
                        g = i + 1
                        dve.wait_ge(k_copied, g + 1)
                        if later(g):
                            dve.wait_ge(scores_ready, CHUNKS * i + CPB)
                        for e in range(2):
                            last = dve.tensor_scalar(kk[0][:, :, e, :], k_full[:], par[:, e:e + 1], None,
                                                     ALU.mult)
                        last.then_inc(k_high, 1)
                        dve.wait_ge(k_high, g + 1)
                        for e in range(2):
                            last = dve.scalar_tensor_tensor(
                                out=kk[1][:, :, e, :], in0=k_full[:], scalar=par[:, e:e + 1],
                                in1=kk[0][:, :, e, :], op0=ALU.mult, op1=ALU.subtract)
                        last.then_inc(k_split, 1)
                    if norm and t == 6:
                        dve.wait_ge(x_loaded, 16 * (i + 3))
                        layer_norm_stats(i + 2, x_in, stats1, mv1, var1, nhalf1, half1, rstd1,
                                         (ln1_stats, ln1_mean, ln1_var, ln1_half, ln1_seed))
                    if out_ and t == 12:
                        split_low(by_tile[1], zT, z_hi, i, z_split)
                    if out_ and t == 7:
                        g = i - 1
                        dve.wait_ge(proj_ready, g + 1)
                        dve.wait_ge(xres_biased, g + 1)
                        if later(g):
                            dve.wait_ge(resid_biased, g)
                        dve.tensor_tensor(resid[:], by_seq[1], x_res[:], ALU.add
                                          ).then_inc(resid_ready, 1)
                        dve.wait_ge(resid_ready, i)
                        layer_norm_stats(i - 1, resid, stats2, mv2, var2, nhalf2, half2, rstd2,
                                         (ln2_stats, ln2_mean, ln2_var, ln2_half, ln2_seed))
                    if ffn and t == 12:
                        g = i - 2
                        dve.wait_ge(down_ready, g + 1)
                        dve.wait_ge(resid_biased, g + 1)
                        if later(g):
                            dve.wait_ge(y_stored, 16 * g)
                        dve.tensor_tensor(y[:], ffn_ps[:, :].rearrange("p (b n) -> p b n", b=GB),
                                          resid_b2[:], ALU.add).then_inc(y_summed, 1)
                    if front and t in (9, 12):
                        g, b = i + 1, (0 if t == 9 else 1)
                        dve.wait_ge(v_ready, g + 1)
                        if later(g):
                            dve.wait_ge(attended, CHUNKS * i + CPB * (b + 1))
                        dve.tensor_tensor(v_aug[:, b, :, 0:HD],
                                          by_seq[0][:, b, :].rearrange("p (h e) -> p h e", h=H),
                                          bvw[:, :].rearrange("p (h e) -> p h e", h=H), ALU.add
                                          ).then_inc(values_set, 1)
                    if front and t == 9:
                        if later(i + 1):
                            dve.wait_ge(scores_masked, CHUNKS * (i + 1))
                        dve.wait_ge(mask_loaded, 16 * (i + 2))
                        dve.tensor_scalar(mask_bias[:], mask_in[:], 1.0, MASKED, ALU.subtract, ALU.mult
                                          ).then_inc(bias_ready, 1)
                    if out_ and t == 10:
                        layer_norm_apply(i - 1, i + 3, resid, mv2, rstd2, xhat2, z_turned, ln2_ready)
                    if attn_ and t == 10:
                        dve.wait_ge(mem_loaded, 16 * (i + 1))
                        if later(i):
                            dve.wait_ge(proj_ready, i)
                        dve.tensor_copy(memT[0][:], mem_in[:]).then_inc(mem_hi, 1)
                        split_low(mem_in[:], memT, mem_hi, i + 1, mem_split)
                    if is_at(i, -2) and t == 10:
                        fold_and_split("q")
                    if norm and t == 10:
                        layer_norm_apply(i + 2, i + 3, x_in, mv1, rstd1, xhat, x_turned, ln1_ready)

            run(dve, iteration, after_first=keys_and_values, after_second=low_parts)

        @block.gpsimd
        def _(pool):
            pool.memset(c1_5[:], 1.5).then_inc(c1_5_set, 1)
            pool.wait_ge(c1_5_set, 1)
            pool.memset(q_stack[96:P].rearrange("p r k n -> p (r k n)").bitcast(F32), 0.0
                        ).then_inc(zeros_set, 1)
            pool.wait_ge(zeros_set, 1)
            pool.memset(k_stack[96:P].rearrange("p r k e s -> p (r k e s)").bitcast(F32), 0.0
                        ).then_inc(zeros_set, 1)
            pool.wait_ge(zeros_set, 2)

            def inverse_root(i):
                steps = (4 * NEWTON_STEPS - 1) * (i + 2)
                for n in range(NEWTON_STEPS):
                    if n:
                        pool.wait_ge(ln_step, steps + 4 * n)
                    pool.tensor_tensor(newton[:], rstds[:], rstds[:], ALU.mult).then_inc(ln_step, 1)
                    pool.wait_ge(ln_step, steps + 4 * n + 1)
                    pool.tensor_tensor(newton[:], newton[:], nhalfs[:], ALU.mult).then_inc(ln_step, 1)
                    pool.wait_ge(ln_step, steps + 4 * n + 2)
                    pool.tensor_tensor(newton[:], newton[:], c1_5[:], ALU.add).then_inc(ln_step, 1)
                    pool.wait_ge(ln_step, steps + 4 * n + 3)
                    last = pool.tensor_tensor(rstds[:], rstds[:], newton[:], ALU.mult)
                    last.then_inc(ln_step if n < NEWTON_STEPS - 1 else ln_rstd, 1)

            def iteration(i, norm, front, attn_, out_, ffn):
                for t in range(TICKS):
                    if attn_ and t < CHUNKS:
                        pool.wait_ge(scores_masked, CHUNKS * i + t + 1)
                        pool.tensor_tensor(scores[:, t], scores[:, t],
                                           row_max[:, t, :].unsqueeze(2).broadcast_to([P, CH, S]),
                                           ALU.subtract).then_inc(scores_shifted, 1)
                    if (norm or out_) and t == 8:
                        if norm:
                            pool.wait_ge(ln1_seed, i + 3)
                        if out_:
                            pool.wait_ge(ln2_seed, i)
                        inverse_root(i)
                    if ffn and t in HIDDEN_TICKS:
                        g, n = i - 2, HIDDEN_TICKS.index(t)
                        pool.wait_ge(hid_hi, HJ * g + n + 1)
                        pool.tensor_tensor(hT[1][:, 2 * n:2 * n + 2, :], hid[:, n % 2],
                                           hT[0][:, 2 * n:2 * n + 2, :], ALU.subtract
                                           ).then_inc(hid_split, 1)
                    if out_ and t == 4:
                        if is_at(i, 1):
                            pool.wait_ge(rows_summed, 1)
                        pool.wait_ge(xres_loaded, 16 * i)
                        pool.tensor_tensor(x_res[:], x_res[:],
                                           bow[:, :].unsqueeze(1).broadcast_to([P, GB, D]),
                                           ALU.add).then_inc(xres_biased, 1)
                    if ffn and t == 2:
                        g = i - 2
                        pool.wait_ge(resid_ready, g + 1)
                        if later(g):
                            pool.wait_ge(y_summed, g)
                        pool.tensor_tensor(resid_b2[:], resid[:],
                                           b2w[:, :].unsqueeze(1).broadcast_to([P, GB, D]),
                                           ALU.add).then_inc(resid_biased, 1)

            run(pool, iteration)

        @block.tensor
        def _(pe):
            def shift_product(name):
                k = KT
                src, shift = SETUP[name][0], (be2c if name == "1" else be1c)
                view = raw(name).rearrange("p (k n) -> p k n", k=k)
                dst = SHIFTS_AT[name]
                pe.wait_ge(weight_loaded[name], 16)
                if name == "v":
                    pe.wait_ge(be1w_set, 1)
                    for j in range(k):
                        last = pe.matmul(dst, be1w[:, j, :], view[:, j, :],
                                         start=(j == 0), stop=(j == k - 1))
                else:
                    for m in range(src.shape[1] // P):
                        for j in range(k):
                            last = pe.matmul(dst[:, m:m + 1], view[:, j, m * P:(m + 1) * P],
                                             shift[:, j:j + 1], start=(j == 0), stop=(j == k - 1))
                last.then_inc(shift_ready, 1)

            def product(dst, pairs, start=True, stop=True, **more):
                n = len(pairs)
                for j, (lhs, rhs) in enumerate(pairs):
                    pe.matmul(dst, lhs[1], rhs[0], start=start and j == 0, stop=False, **more)
                    pe.matmul(dst, lhs[0], rhs[1], start=False, stop=False, **more)
                    last = pe.matmul(dst, lhs[0], rhs[0], start=False, stop=stop and j == n - 1, **more)
                return last

            def cut(pair, *at):
                return pair[0][at], pair[1][at]

            ALL = slice(None)

            def seq(b):
                return slice(b * S, (b + 1) * S)

            def turn(dst, src):
                for k in range(KT):
                    for b in range(GB):
                        last = pe.transpose(dst[:, k, seq(b)], src[:, b, k * P:(k + 1) * P], ident[:])
                return last

            def up(i, t):
                g, n = i - 2, UP_TICKS.index(t)
                if is_at(i, 2) and n == 0:
                    pe.wait_ge(split_lo, SPLIT_AT["2"])
                if n == 0:
                    pe.wait_ge(z_split, g + 1)
                    if later(g):
                        pe.wait_ge(y_summed, g)
                else:
                    pe.wait_ge(hid_relu, HJ * g + n)
                for j in range(2):
                    f = 2 * n + j
                    last = product(ffn_ps[:, j * ROWS:(j + 1) * ROWS],
                                   [(cut(w1, ALL, k, slice(f * P, (f + 1) * P)), cut(zT, ALL, k))
                                    for k in range(KT)])
                last.then_inc(hid_ready, 1)

            def scores_of(i, n):
                b, c = divmod(n, CPB)
                if b == 0:
                    if c == 0:
                        pe.wait_ge(q_stacked, 16 * TERMS * CPB * (i + 1))
                    pe.wait_ge(k_stacked[c], 16 * TERMS * (i + 1))
                if n >= 2 or later(i):
                    pe.wait_ge(scores_masked, CHUNKS * i + n - 1)
                for k in range(KT):
                    last = pe.matmul(score_ps[n % 2][:, k * 2 * S:(k + 1) * 2 * S],
                                     q_stack[:, c, k, seq(b)],
                                     k_stack[:, c, GB * k + b].rearrange("p e s -> p (e s)"),
                                     start=True, stop=True)
                last.then_inc(scores_ready, 1)

            def values_of(i, n):
                pe.wait_ge(probs_ready, CHUNKS * i + n + 2)
                if n == 0:
                    pe.wait_ge(values_set, GB * (i + 1))
                if n % CPB == 0 and (n or later(i)):
                    pe.wait_ge(attn_copied, GB * i + n // CPB)
                for k in (n, n + 1):
                    b, c = divmod(k, CPB)
                    for h in range(CH):
                        last = pe.matmul(value_ps[SLOT * h:SLOT * (h + 1), c * S:(c + 1) * S],
                                         v_aug[:, b, head_of(c, h), :],
                                         probs[:, c, h * S:(h + 1) * S], start=True, stop=True)
                    last.then_inc(attended, 1)

            def heads_turned(i, b):
                pe.wait_ge(attn_copied, GB * (i - 1) + b + 1)
                for c in range(CPB):
                    last = pe.transpose(work[b][:, c * S:(c + 1) * S],
                                        attn_aug[:, b, c * S:(c + 1) * S], ident[:])
                last.then_inc(attn_turned, 1)

            def iteration(i, norm, front, attn_, out_, ffn):
                fronts, outs = stages_before(i)
                for t in range(TICKS):
                    if attn_ and t == 0:
                        scores_of(i, 0)
                        scores_of(i, 1)
                    if attn_ and t in SCORE_TICKS:
                        scores_of(i, SCORE_TICKS[t])
                    if attn_ and 0 <= t - TURN_LAG < CHUNKS:
                        k = t - TURN_LAG
                        pe.wait_ge(scores_shifted, CHUNKS * i + k + 1)
                        if k >= 2 or later(i):
                            pe.wait_ge(probs_ready, CHUNKS * i + k - 1)
                        for h in range(CH):
                            last = pe.transpose(turn_ps[k % 2][:, h * S:(h + 1) * S], scores[:, k, h, :],
                                                ident[:])
                        last.then_inc(scores_turned, 1)
                    if attn_ and t in VALUE_TICKS[:3]:
                        values_of(i, 2 * VALUE_TICKS.index(t))
                    if front and t == 0:
                        pe.wait_ge(ln1_ready, i + 2)
                        if not isinstance(i, int) or outs > 0:
                            pe.wait_ge(z_split, outs)
                        turn(by_tile[1], xhat).then_inc(x_turned, 1)
                    if out_ and t == 0:
                        pe.wait_ge(values_set, GB * fronts)
                        heads_turned(i, 0)
                    if ffn and t in UP_TICKS:
                        up(i, t)
                    if attn_ and t == 1:
                        scores_of(i, 2)
                    if out_ and t == 1:
                        if front:
                            pe.wait_ge(x_split, i + 2)
                        else:
                            pe.wait_ge(z_split, outs)
                        heads_turned(i, 1)
                    if out_ and t == 2:
                        pe.wait_ge(attn_normed, GB * i)
                        turn(by_tile[1], attn).then_inc(attnT_ready, 1)
                    if front and t in (1, 3):
                        which = t // 2
                        if which == 1:
                            pe.wait_ge(q_split, i + 2)
                        else:
                            pe.wait_ge(x_split, i + 2)
                            if out_:
                                pe.wait_ge(attn_normed, GB * i - 1)
                            elif fronts > 0:
                                pe.wait_ge(values_set, GB * fronts)
                        if is_at(i, -1):
                            pe.wait_ge(split_lo, SPLIT_AT["qk"[which]])
                        for m in range(KT):
                            last = product(by_tile[0][:, m, :],
                                           [(cut((wq, wk)[which], ALL, k, slice(m * P, (m + 1) * P)),
                                             cut(xT, ALL, k)) for k in range(KT)])
                        last.then_inc((q_ready, k_ready)[which], 1)
                    if out_ and t in (5, 6):
                        b = t - 5
                        if is_at(i, 1) and b == 0:
                            pe.wait_ge(split_lo, SPLIT_AT["g"])
                        if b == 0:
                            pe.wait_ge(attnT_split, i)
                            pe.wait_ge(mem_split, i)
                        last = product(by_seq[1][:, b, :],
                                       [(cut(attnT, ALL, k, seq(b)), cut(wo, ALL, k)) for k in range(KT)]
                                       + [(cut(memT, ALL, k, seq(b)), cut(wg, ALL, k)) for k in range(KT)])
                        if b == GB - 1:
                            last.then_inc(proj_ready, 1)
                    if front and t == 8:
                        if is_at(i, -1):
                            pe.wait_ge(split_lo, SPLIT_AT["v"])
                        pe.wait_ge(k_copied, i + 2)
                        for b in range(GB):
                            last = product(by_seq[0][:, b, :],
                                           [(cut(xT, ALL, k, seq(b)), cut(wv, ALL, k)) for k in range(KT)])
                        last.then_inc(v_ready, 1)
                    if out_ and t == 11:
                        pe.wait_ge(ln2_ready, i)
                        pe.wait_ge(resid_ready, i)
                        turn(by_tile[1], xhat2).then_inc(z_turned, 1)
                    if ffn and t in DOWN_TICKS:
                        g, part = i - 2, DOWN_TICKS.index(t)
                        if part == 0:
                            pe.wait_ge(hid_relu, HJ * g + HJ)
                        pe.wait_ge(hid_split, HJ * g + part + 1)
                        for f in range(2 * part, 2 * part + 2):
                            for b in range(GB):
                                last = product(ffn_ps[:, b * D:(b + 1) * D],
                                               [(cut(hT, ALL, f, seq(b)), cut(w2, ALL, f))],
                                               start=(f == 0 and b == 0), stop=(f == FT - 1),
                                               skip_group_check=True)
                        if part == HJ - 1:
                            last.then_inc(down_ready, 1)
                    if attn_ and t == VALUE_TICKS[3]:
                        values_of(i, 6)

            pe.wait_ge(vec_loaded, 16)
            for name in "qkv":
                shift_product(name)
            pe.wait_ge(ident_loaded, 16)
            pe.wait_ge(zeros_set, 2)
            run(pe, iteration, after_second=lambda: shift_product("1"))


def kernel(**inputs):
    import numpy as np
    import concourse.bacc as bacc
    from concourse.bass_utils import run_bass_kernel_spmd

    nc = bacc.Bacc("TRN2", target_bir_lowering=False, num_devices=1)
    arrays, args = {}, []

    def give(name, a):
        arrays[name] = np.ascontiguousarray(a)
        args.append(nc.dram_tensor(name, arrays[name].shape, mybir.dt.from_np(arrays[name].dtype),
                                   kind="ExternalInput").ap())

    give("x_dram", inputs["x"])
    give("memory_dram", np.asarray(inputs["ctx_1024"]).reshape(-1, inputs["ctx_1024"].shape[-1]).T)
    give("mask_dram", inputs["mask_BxSxS2_fk0"])
    order = [16 * head_of(c, h) + e for c in range(4) for h in range(4) for e in range(16)]
    for n in ("Wq", "Wk", "Wv", "Wo", "Wg", "W1", "W2"):
        wT = np.asarray(inputs[f"L0_xattn_{n}"]).T
        give(f"{n}T_dram", wT[order] if n == "Wo" else wT)
    rows = np.arange(P) // 16 % 2
    vectors = {"even_odd": np.stack([rows == 0, rows == 1], axis=1).astype(np.float32)}
    for n, cols in VECTORS[:-1]:
        vectors[n] = np.asarray(inputs[f"L0_xattn_{n}"]).reshape(cols, P).T
    give("vectors_dram", np.concatenate([vectors[n] for n, _ in VECTORS], axis=1))
    give("rows_dram", np.concatenate([np.asarray(inputs[f"L0_xattn_{n}"]) for n in ("bv", "bo", "bg", "b2")]))
    give("identity_dram", np.eye(P, dtype=np.float32))
    shape = tuple(inputs["x"].shape)
    args.append(nc.dram_tensor("out_dram", shape, F32, kind="ExternalOutput").ap())
    xattn_block(nc, *args)
    r = run_bass_kernel_spmd(nc, [arrays], core_ids=[0])
    return r.results[0]["out_dram"]
```

```python
from contextlib import ExitStack

import concourse.bass as bass
from concourse import mybir

ALU = mybir.AluOpType
ACT = mybir.ActivationFunctionType
F32 = mybir.dt.float32
F32R = mybir.dt.float32r
I32 = mybir.dt.int32

P = 128
EPS = 1e-5
MASKED = 1e9
HIGHEST = 3.0e38
RSQRT_SEED = float(0x5F3759DF)
NEWTON_STEPS = 3

TICKS = 13
SCORE_TICKS = {2: 3, 3: 4, 5: 5, 6: 6, 7: 7}
EXP_TICKS = (0, 1, 2, 3, 5, 6, 7, 9)
INVERT_TICKS = (1, 2, 3, 5, 5, 7, 7, 9)
NORM_TICKS = (1, 2, 3, 5, 6, 7, 8, 9)
TURN_TICKS = (3, 4, 5, 7, 9, 10, 12)
UP_TICKS = (0, 2, 4, 7)
RELU_TICKS = (0, 3, 5, 7)
HIDDEN_TICKS = (1, 3, 5, 8)
DOWN_TICKS = (9, 10, 11, 12)


VECTORS = (("g1", 2), ("be1", 2), ("g2", 2), ("be2", 2), ("bq", 2), ("bk", 2), ("b1", 8), ("even_odd", 2))


def later(g):
    return not (isinstance(g, int) and g == 0)


def is_at(i, n):
    return isinstance(i, int) and i == n


def head_of(c, h):
    return 8 * (h // 2) + 2 * c + h % 2


def xattn_block(nc, x, memory, mask, wqT, wkT, wvT, woT, wgT, w1T, w2T,
                vectors, rows, identity, out):
    B, S, D = x.shape
    FF = w1T.shape[1]
    H = 16
    HD = D // H
    GB = 2
    GROUPS = B // GB
    ROWS = GB * S
    KT = D // P
    FT = FF // P
    CH = 4
    CPB = H // CH
    CHUNKS = GB * CPB
    HJ = FT // 2
    assert S == P and D == 2 * P and CHUNKS == 8 and HJ == 4

    x_rows = x.rearrange("(g b) s d -> g s b d", b=GB)
    mem_cols = memory.rearrange("(k p) (g r) -> g p k r", p=P, r=ROWS)
    mask_rows = mask.rearrange("(g b) s t -> g s b t", b=GB)
    out_rows = out.rearrange("(g b) s d -> g s b d", b=GB)

    with ExitStack() as ctx:
        def sb(name, shape, dt=F32):
            return ctx.enter_context(nc.sbuf_tensor(name, shape, dt))

        def bank(name):
            return ctx.enter_context(nc.psum_tensor(name, [P, 512], F32))

        def sem(name):
            return ctx.enter_context(nc.semaphore(name))

        ident = sb("ident", [P, P])
        vector_cols, at = {}, 0
        vec = sb("vec", [P, sum(n for _, n in VECTORS)])
        for name, n in VECTORS:
            vector_cols[name] = vec[:, at:at + n]
            at += n
        g1c, be1c, g2c, be2c, bqc, bkc, b1c, par = (vector_cols[name] for name, _ in VECTORS)
        row = sb("row", [P, 4, D])
        bvw, bow, bgw, b2w = (row[:, n, :] for n in range(4))
        be1w = sb("be1w", [P, KT, P])
        weights = {}
        for n, cols in (("q", KT * D), ("k", KT * D), ("v", KT * D), ("o", KT * D), ("g", KT * D),
                        ("1", KT * FF), ("2", FT * D)):
            weights[n] = (sb(f"w{n}_hi", [P, cols], F32R), sb(f"w{n}_lo", [P, cols], F32R))

        def tiles(n, k):
            return [w[:, :].rearrange("p (k n) -> p k n", k=k) for w in weights[n]]

        wq, wk, wv, wo, wg = (tiles(n, KT) for n in "qkvog")
        w1, w2 = tiles("1", KT), tiles("2", FT)

        x_in = sb("x_in", [P, GB, D])
        stats1, mv1 = sb("stats1", [P, GB, 6]), sb("mv1", [P, GB, 2])
        var1, half1 = sb("var1", [P, GB]), sb("half1", [P, GB], I32)
        xhat = sb("xhat", [P, GB, D])
        xT = [sb("xT_hi", [P, KT, ROWS], F32R), sb("xT_lo", [P, KT, ROWS], F32R)]
        q = [sb("q_hi", [P, KT, ROWS], F32R), sb("q_lo", [P, KT, ROWS], F32R)]
        k_full = sb("k_full", [P, KT * GB, S])
        kk = [sb("k_hi", [P, KT * GB, 2, S], F32R), sb("k_lo", [P, KT * GB, 2, S], F32R)]
        q_stack = sb("q_stack", [P, CPB, KT, ROWS], F32R)
        k_stack = sb("k_stack", [P, CPB, KT * GB, 2, S], F32R)
        v_pad = sb("v_pad", [P, GB, H, 2 * HD])
        mask_in, mask_bias = sb("mask_in", [P, GB, S]), sb("mask_bias", [P, GB, S])
        scores = sb("scores", [P, CHUNKS, CH, S])
        row_min = sb("row_min", [P, CHUNKS, CH])
        row_sum, sum_inv = sb("row_sum", [P, CHUNKS, CH]), sb("sum_inv", [P, CHUNKS, CH])
        carrier = sb("carrier", [P, CHUNKS])
        probs = sb("probs", [P, CPB, CH * S])
        attnT = [sb("attnT_hi", [P, KT, ROWS], F32R), sb("attnT_lo", [P, KT, ROWS], F32R)]
        mem_in = sb("mem_in", [P, KT, ROWS])
        memT = [sb("memT_hi", [P, KT, ROWS], F32R), sb("memT_lo", [P, KT, ROWS], F32R)]
        x_res = sb("x_res", [P, GB, D])
        resid = sb("resid", [P, GB, D])
        stats2, mv2 = sb("stats2", [P, GB, 6]), sb("mv2", [P, GB, 2])
        var2, half2 = sb("var2", [P, GB]), sb("half2", [P, GB], I32)
        rstd1, rstd2 = sb("rstd1", [P, GB]), sb("rstd2", [P, GB])
        nhalf1, nhalf2 = sb("nhalf1", [P, GB]), sb("nhalf2", [P, GB])
        newton1, newton2 = sb("newton1", [P, GB]), sb("newton2", [P, GB])
        c1_5 = sb("c1_5", [P, GB])
        xhat2 = sb("xhat2", [P, GB, D])
        zT = [sb("zT_hi", [P, KT, ROWS], F32R), sb("zT_lo", [P, KT, ROWS], F32R)]
        resid_b2 = sb("resid_b2", [P, GB, D])
        hid = sb("hid", [P, 2, 2, ROWS])
        hT = [sb("hT_hi", [P, FT, ROWS], F32R), sb("hT_lo", [P, FT, ROWS], F32R)]
        y = sb("y", [P, GB, D])

        score_ps = [bank("score_ps0"), bank("score_ps1")]
        turn_ps = [bank("turn_ps0"), bank("turn_ps1")]
        value_ps = bank("value_ps")
        ffn_ps = bank("ffn_ps")
        work = [bank("work_ps0"), bank("work_ps1")]
        by_tile = [w[:, :].rearrange("p (k r) -> p k r", k=KT) for w in work]
        value_tiles = value_ps[:, :].rearrange("p (k r) -> p k r", k=KT)
        by_seq = [w[:, :].rearrange("p (b n) -> p b n", b=GB) for w in work]

        vec_loaded, row_loaded, ident_loaded = sem("vec_loaded"), sem("row_loaded"), sem("ident_loaded")
        weight_loaded = {n: sem(f"w{n}_loaded") for n in "qkvog12"}
        folded, up_folded = sem("folded"), sem("up_folded")
        split_hi, weights_hi, split_lo = sem("split_hi"), sem("weights_hi"), sem("split_lo")
        rows_summed, c1_5_set = sem("rows_summed"), sem("c1_5_set")
        shift_ready, shift_added = sem("shift_ready"), sem("shift_added")
        pads_set, be1w_set = sem("pads_set"), sem("be1w_set")
        x_loaded, mem_loaded, mask_loaded = sem("x_loaded"), sem("mem_loaded"), sem("mask_loaded")
        xres_loaded, y_stored = sem("xres_loaded"), sem("y_stored")
        ln1_stats, ln1_mean, ln1_var, ln1_half, ln1_seed, ln1_ready = (
            sem(f"ln1_{n}") for n in ("stats", "mean", "var", "half", "seed", "ready"))
        x_turned, x_hi, x_split = sem("x_turned"), sem("x_hi"), sem("x_split")
        q_ready, q_high, q_split = sem("q_ready"), sem("q_high"), sem("q_split")
        k_ready, k_copied, k_high, k_split = sem("k_ready"), sem("k_copied"), sem("k_high"), sem("k_split")
        zeros_set = sem("zeros_set")
        q_stacked, k_stacked = sem("q_stacked"), [sem(f"k_stacked{r}") for r in range(CPB)]
        v_ready, values_set, bias_ready = sem("v_ready"), sem("values_set"), sem("bias_ready")
        scores_ready, scores_masked = sem("scores_ready"), sem("scores_masked")
        exps_ready, sums_inverted, probs_normed = sem("exps_ready"), sem("sums_inverted"), sem("probs_normed")
        probs_turned, probs_copied = sem("probs_turned"), sem("probs_copied")
        attended = sem("attended")
        attnT_hi, attnT_split = sem("s_attnT_hi"), sem("attnT_split")
        mem_hi, mem_split = sem("mem_hi"), sem("mem_split")
        proj_ready, xres_biased, resid_ready = sem("proj_ready"), sem("xres_biased"), sem("resid_ready")
        ln2_stats, ln2_mean, ln2_var, ln2_half, ln2_seed, ln2_ready = (
            sem(f"ln2_{n}") for n in ("stats", "mean", "var", "half", "seed", "ready"))
        z_turned, z_hi, z_split = sem("z_turned"), sem("z_hi"), sem("z_split")
        ln1_step, ln1_rstd, ln2_step, ln2_rstd = (sem(n) for n in ("ln1_step", "ln1_rstd", "ln2_step", "ln2_rstd"))
        hid_ready, hid_relu, hid_hi, hid_split = (sem(f"s_hid_{n}") for n in ("ready", "relu", "hi", "split"))
        down_ready, resid_biased, y_summed = sem("down_ready"), sem("resid_biased"), sem("y_summed")

        def stages_before(i):
            if isinstance(i, int):
                return min(max(i + 1, 0), GROUPS), min(max(i - 1, 0), GROUPS)
            return i + 1, i - 1

        def run(eng, iteration, ahead=2, after_first=None, after_second=None):
            def peeled(i):
                iteration(i, *(0 <= g < GROUPS for g in (i + 2, i + 1, i, i - 1, i - 2)))
            for i in range(-2, 3):
                peeled(i)
                if i == -2 and after_first is not None:
                    after_first()
                if i == -1 and after_second is not None:
                    after_second()
            with eng.Fori(3, GROUPS - ahead) as i:
                iteration(i, True, True, True, True, True)
            for i in range(GROUPS - ahead, GROUPS + 2):
                peeled(i)

        SETUP = {"q": (wqT, KT), "k": (wkT, KT), "v": (wvT, KT), "o": (woT, KT), "g": (wgT, KT),
                 "1": (w1T, KT), "2": (w2T, FT)}
        SPLIT_AT = {n: j + 1 for j, n in enumerate(SETUP)}
        SHIFTED = "qkv1"
        SHIFTS_AT = {"q": ffn_ps[:, 0:KT], "k": score_ps[0][:, 0:KT], "v": score_ps[1][:, 0:D],
                     "1": value_ps[:, 0:FT]}
        TERMS = 3

        def raw(name):
            if name == "2":
                return probs[:].rearrange("p c n -> p (c n)")
            if name == "g":
                return y[:].rearrange("p b n -> p (b n)")
            at, n = {"q": (0, 1), "k": (1, 1), "v": (2, 1), "o": (3, 1), "1": (4, 4)}[name]
            return scores[:, at:at + n].rearrange("p t h s -> p (t h s)")

        block = ctx.enter_context(nc.Block())

        @block.sync
        def _(sp):
            def load_weight(name):
                src, k = SETUP[name]
                sp.dma_start(raw(name).rearrange("p (k n) -> p k n", k=k),
                             src.rearrange("(k p) n -> p k n", p=P)).then_inc(weight_loaded[name], 16)

            sp.dma_start(x_in[:], x_rows[0]).then_inc(x_loaded, 16)
            sp.dma_start(vec[:], vectors).then_inc(vec_loaded, 16)
            load_weight("q")
            sp.dma_start(ident[:], identity).then_inc(ident_loaded, 16)
            load_weight("k")
            load_weight("v")
            sp.dma_start(row[:].rearrange("p n d -> p (n d)"),
                         rows.rearrange("(a d) -> a d", a=1).broadcast_to([P, 4 * D])
                         ).then_inc(row_loaded, 16)
            sp.dma_start(mask_in[:], mask_rows[0]).then_inc(mask_loaded, 16)
            load_weight("o")
            load_weight("g")
            sp.dma_start(mem_in[:], mem_cols[0]).then_inc(mem_loaded, 16)
            sp.dma_start(x_res[:], x_rows[0]).then_inc(xres_loaded, 16)
            load_weight("1")
            load_weight("2")

            def known(i, low, high):
                return not isinstance(i, int) or low <= i < high

            def iteration(i, norm, front, attn_, out_, ffn):
                if front:
                    sp.wait_ge(q_split, i + 2)
                    for r in range(CPB):
                        if later(i + 1):
                            sp.wait_ge(scores_ready, CHUNKS * i + CPB + r + 1)
                        for j, high_low in enumerate((1, 0, 0)):
                            sp.dma_start(q_stack[32 * j:32 * j + 32, r].bitcast(F32),
                                         q[high_low][32 * r:32 * r + 32].bitcast(F32)
                                         ).then_inc(q_stacked, 16)
                    if known(i, 1, GROUPS):
                        sp.wait_ge(mem_split, i)
                        sp.dma_start(mem_in[:], mem_cols[i]).then_inc(mem_loaded, 16)
                    sp.wait_ge(k_split, i + 2)
                    for r in range(CPB):
                        for j, high_low in enumerate((0, 1, 0)):
                            sp.dma_start(k_stack[32 * j:32 * j + 32, r].bitcast(F32),
                                         kk[high_low][32 * r:32 * r + 32].bitcast(F32)
                                         ).then_inc(k_stacked[r], 16)
                if is_at(i, GROUPS - 1):
                    sp.wait_ge(mem_split, i)
                    sp.dma_start(mem_in[:], mem_cols[i]).then_inc(mem_loaded, 16)
                if known(i, 1, GROUPS):
                    sp.wait_ge(resid_ready, i)
                    sp.dma_start(x_res[:], x_rows[i]).then_inc(xres_loaded, 16)
                if known(i, -1, GROUPS - 2):
                    sp.wait_ge(bias_ready, i + 2)
                    sp.dma_start(mask_in[:], mask_rows[i + 2]).then_inc(mask_loaded, 16)
                if known(i, -2, GROUPS - 3):
                    sp.wait_ge(ln1_ready, i + 3)
                    sp.dma_start(x_in[:], x_rows[i + 3]).then_inc(x_loaded, 16)
                if ffn:
                    sp.wait_ge(y_summed, i - 1)
                    sp.dma_start(out_rows[i - 2], y[:]).then_inc(y_stored, 16)

            run(sp, iteration, ahead=3)
            sp.wait_ge(y_stored, 16 * GROUPS)

        @block.scalar
        def _(act):
            act.wait_ge(vec_loaded, 16)
            act.wait_ge(ident_loaded, 16)
            for k in range(KT):
                last = act.activation(be1w[:, k, :], ident[:], ACT.Identity, bias=be1c[:, k:k + 1],
                                      scale=0.0)
            last.then_inc(be1w_set, 1)

            def split_high(src, dst, ready, count, free, freed, done):
                act.wait_ge(ready, count)
                if freed is not None:
                    act.wait_ge(free, freed)
                act.activation(dst[:], src, ACT.Copy).then_inc(done, 1)

            def exponentials(i, k):
                act.wait_ge(scores_masked, CHUNKS * i + k + 1)
                for h in range(CH):
                    last = act.activation(scores[:, k, h, :], scores[:, k, h, :], ACT.Exp,
                                          bias=row_min[:, k, h:h + 1], scale=-1.0,
                                          accum_out=row_sum[:, k, h:h + 1])
                last.then_inc(exps_ready, 1)

            def copy_turned(g, k):
                act.wait_ge(probs_turned, CHUNKS * g + k + 1)
                if k >= CPB or later(g):
                    act.wait_ge(attended, GB * g + k // CPB)
                act.activation(probs[:, k % CPB, :], turn_ps[k % 2][:, :], ACT.Copy
                               ).then_inc(probs_copied, 1)

            def iteration(i, norm, front, attn_, out_, ffn):
                for t in range(TICKS):
                    if out_ and t == 0:
                        copy_turned(i - 1, CHUNKS - 1)
                    if front and t == 0:
                        g = i + 1
                        split_high(by_tile[1], xT[0], x_turned, g + 1, v_ready,
                                   g if later(g) else None, x_hi)
                    if attn_ and t == EXP_TICKS[0]:
                        exponentials(i, 0)
                    if is_at(i, 2) and t == 0:
                        act.wait_ge(shift_added, 4)
                    if attn_ and t == 7:
                        copy_turned(i, TURN_TICKS.index(t))
                    if ffn and t in RELU_TICKS:
                        g, n = i - 2, RELU_TICKS.index(t)
                        act.wait_ge(hid_ready, HJ * g + n + 1)
                        if n >= 2 or later(g):
                            act.wait_ge(hid_split, HJ * g + n - 1)
                        for j in range(2):
                            last = act.activation(hid[:, n % 2, j, :], ffn_ps[:, j * ROWS:(j + 1) * ROWS],
                                                  ACT.Relu, bias=b1c[:, 2 * n + j:2 * n + j + 1])
                        last.then_inc(hid_relu, 1)
                    if attn_ and t in TURN_TICKS and t != 7:
                        copy_turned(i, TURN_TICKS.index(t))
                    if out_ and t == 12:
                        g = i - 1
                        split_high(by_tile[1], zT[0], z_turned, g + 1, hid_ready,
                                   HJ * g if later(g) else None, z_hi)
                    if front and t == 2:
                        g = i + 1
                        if not later(g):
                            act.wait_ge(shift_added, 2)
                        act.wait_ge(q_ready, g + 1)
                        if later(g):
                            act.wait_ge(q_stacked, 16 * TERMS * CPB * g)
                        for k in range(KT):
                            last = act.activation(q[0][:, k, :], by_tile[1][:, k, :], ACT.Identity,
                                                  bias=bqc[:, k:k + 1])
                        last.then_inc(q_high, 1)
                    if front and t == 3:
                        g = i + 1
                        act.wait_ge(k_ready, g + 1)
                        if later(g):
                            act.wait_ge(k_split, g)
                        for k in range(KT):
                            last = act.activation(
                                k_full[:, GB * k:GB * (k + 1), :].rearrange("p b s -> p (b s)"),
                                by_tile[0][:, k, :], ACT.Identity, bias=bkc[:, k:k + 1])
                        last.then_inc(k_copied, 1)
                    if attn_ and t in EXP_TICKS[1:]:
                        exponentials(i, EXP_TICKS.index(t))

            def high_parts():
                for n, name in enumerate("og12"):
                    act.wait_ge(weight_loaded[name], 16)
                    if name == "1":
                        act.wait_ge(shift_ready, len(SHIFTED))
                        w = raw("1").rearrange("p (k n) -> p k n", k=KT)
                        for k in range(KT):
                            last = act.activation(w[:, k, :], w[:, k, :], ACT.Copy, scale=g2c[:, k:k + 1])
                        last.then_inc(up_folded, 1)
                        act.wait_ge(up_folded, 1)
                    act.activation(weights[name][0][:], raw(name), ACT.Copy).then_inc(weights_hi, 1)

            run(act, iteration, after_second=high_parts)

        @block.vector
        def _(dve):
            dve.memset(v_pad[:], 0.0).then_inc(pads_set, 1)
            dve.wait_ge(vec_loaded, 16)
            dve.wait_ge(pads_set, 1)

            def add_shift(name):
                dst = {"q": bqc, "k": bkc, "v": bvw, "1": b1c}[name]
                dve.wait_ge(shift_ready, SHIFTED.index(name) + 1)
                if name == "v":
                    dve.wait_ge(row_loaded, 16)
                add = dve.tensor_tensor(dst, SHIFTS_AT[name], dst, ALU.add)
                if name != "q":
                    add.then_inc(shift_added, 1)
                    return
                add.then_inc(folded, 1)
                dve.wait_ge(folded, 1)
                dve.tensor_scalar(bqc, bqc, -HD ** -0.5, None, ALU.mult).then_inc(shift_added, 1)

            def low_part(name):
                dve.tensor_tensor(weights[name][1][:], raw(name), weights[name][0][:], ALU.subtract
                                  ).then_inc(split_lo, 1)

            def fold_and_split(name):
                dve.wait_ge(weight_loaded[name], 16)
                add_shift(name)
                view = raw(name).rearrange("p (k n) -> p k n", k=KT)
                for j in range(KT):
                    last = dve.tensor_scalar(view[:, j, :], view[:, j, :], g1c[:, j:j + 1],
                                             -HD ** -0.5 if name == "q" else 1.0, ALU.mult, ALU.mult)
                last.then_inc(folded, 1)
                n = SHIFTED.index(name)
                dve.wait_ge(folded, n + 2)
                dve.tensor_copy(weights[name][0][:], raw(name)).then_inc(split_hi, 1)
                dve.wait_ge(split_hi, n + 1)
                low_part(name)

            def keys_and_values():
                fold_and_split("k")
                fold_and_split("v")

            def low_parts():
                dve.tensor_tensor(bow, bow, bgw, ALU.add).then_inc(rows_summed, 1)
                add_shift("1")
                for n, name in enumerate("og12"):
                    dve.wait_ge(weights_hi, n + 1)
                    low_part(name)

            def layer_norm_stats(g, src, stats, mv, var, nhalf, half, rstd, sems):
                stats_done, mean_done, var_done, half_done, seed_done = sems
                for b in range(GB):
                    last = dve.bn_stats(stats[:, b, :], src[:, b, :])
                last.then_inc(stats_done, 1)
                dve.wait_ge(pads_set, 1)
                dve.wait_ge(stats_done, g + 1)
                for b in range(GB):
                    last = dve.bn_aggr(mv[:, b, :], stats[:, b, :])
                last.then_inc(mean_done, 1)
                dve.wait_ge(mean_done, g + 1)
                dve.tensor_scalar(var[:], mv[:, :, 1], EPS, None, ALU.add).then_inc(var_done, 1)
                dve.tensor_scalar(nhalf[:], mv[:, :, 1], EPS, -0.5, ALU.add, ALU.mult)
                dve.wait_ge(var_done, g + 1)
                dve.tensor_scalar(half[:], var[:].bitcast(I32), 1, None, ALU.logical_shift_right
                                  ).then_inc(half_done, 1)
                dve.wait_ge(half_done, g + 1)
                dve.tensor_scalar(rstd[:].bitcast(I32), half[:], -1.0, RSQRT_SEED, ALU.mult, ALU.add
                                  ).then_inc(seed_done, 1)

            def inverse_root(g):
                dve.wait_ge(ln2_seed, g + 1)
                steps = (3 * NEWTON_STEPS - 1) * g
                for n in range(NEWTON_STEPS):
                    if n:
                        dve.wait_ge(ln2_step, steps + 3 * n)
                    dve.tensor_tensor(newton2[:], rstd2[:], rstd2[:], ALU.mult).then_inc(ln2_step, 1)
                    dve.wait_ge(ln2_step, steps + 3 * n + 1)
                    dve.tensor_tensor(newton2[:], newton2[:], nhalf2[:], ALU.mult).then_inc(ln2_step, 1)
                    dve.wait_ge(ln2_step, steps + 3 * n + 2)
                    last = dve.scalar_tensor_tensor(out=rstd2[:], in0=newton2[:], scalar=1.5, in1=rstd2[:],
                                                    op0=ALU.add, op1=ALU.mult)
                    last.then_inc(ln2_step if n < NEWTON_STEPS - 1 else ln2_rstd, 1)

            def layer_norm_apply(g, src, mv, rstd, rstd_done, dst, free, done):
                dve.wait_ge(rstd_done, g + 1)
                if later(g):
                    dve.wait_ge(free, g)
                for b in range(GB):
                    last = dve.tensor_scalar(dst[:, b, :], src[:, b, :], mv[:, b, 0:1],
                                             rstd[:, b:b + 1], ALU.subtract, ALU.mult)
                last.then_inc(done, 1)

            def invert_sums(i, k):
                dve.wait_ge(exps_ready, CHUNKS * i + k + 1)
                dve.reciprocal(sum_inv[:, k, :], row_sum[:, k, :]).then_inc(sums_inverted, 1)

            def set_values(g, b):
                dve.wait_ge(v_ready, g + 1)
                if later(g):
                    dve.wait_ge(attended, GB * (g - 1) + b + 1)
                for e in range(2):
                    def heads(rows):
                        return rows.rearrange("p (j e d) -> p j e d", e=2, d=HD)[:, :, e, :]
                    last = dve.tensor_tensor(
                        v_pad[:, b].rearrange("p (j e) d -> p j e d", e=2)[:, :, e, HD * e:HD * (e + 1)],
                        heads(by_seq[0][:, b, :]), heads(bvw), ALU.add)
                last.then_inc(values_set, 1)

            def split_low(src, halves, high, count, done):
                dve.wait_ge(high, count)
                dve.tensor_tensor(halves[1][:], src, halves[0][:], ALU.subtract).then_inc(done, 1)

            def iteration(i, norm, front, attn_, out_, ffn):
                for t in range(TICKS):
                    if attn_ and t == 7:
                        invert_sums(i, INVERT_TICKS.index(t))
                    if out_ and t == 7:
                        g = i - 1
                        dve.wait_ge(proj_ready, g + 1)
                        dve.wait_ge(xres_biased, g + 1)
                        if later(g):
                            dve.wait_ge(resid_biased, g)
                        dve.tensor_tensor(resid[:], by_seq[1], x_res[:], ALU.add
                                          ).then_inc(resid_ready, 1)
                        dve.wait_ge(resid_ready, i)
                        layer_norm_stats(i - 1, resid, stats2, mv2, var2, nhalf2, half2, rstd2,
                                         (ln2_stats, ln2_mean, ln2_var, ln2_half, ln2_seed))
                    if out_ and t == 12:
                        split_low(by_tile[1], zT, z_hi, i, z_split)
                    if ffn and t == 12:
                        g = i - 2
                        dve.wait_ge(down_ready, g + 1)
                        dve.wait_ge(resid_biased, g + 1)
                        if later(g):
                            dve.wait_ge(y_stored, 16 * g)
                        dve.tensor_tensor(y[:], ffn_ps[:, :].rearrange("p (b n) -> p b n", b=GB),
                                          resid_b2[:], ALU.add).then_inc(y_summed, 1)
                    if attn_ and t < CHUNKS:
                        b = t // CPB
                        if t == 0:
                            dve.wait_ge(bias_ready, i + 1)
                        if later(i):
                            dve.wait_ge(probs_turned, CHUNKS * (i - 1) + t + 1)
                        dve.wait_ge(scores_ready, CHUNKS * i + t + 1)
                        dve.memset(carrier[:, t:t + 1], 0.0)
                        for h in range(CH):
                            last = dve.tensor_tensor_reduce(
                                out=scores[:, t, h, :], in0=score_ps[t % 2][:, h * S:(h + 1) * S],
                                in1=mask_bias[:, b, :], scale=1.0, scalar=HIGHEST, op0=ALU.add,
                                op1=ALU.min, accum_out=row_min[:, t, h:h + 1])
                        last.then_inc(scores_masked, 1)
                    if front and t == 0:
                        split_low(by_tile[1], xT, x_hi, i + 2, x_split)
                    if out_ and t == 1:
                        g = i - 1
                        dve.wait_ge(mem_loaded, 16 * (g + 1))
                        if later(g):
                            dve.wait_ge(proj_ready, g)
                        dve.tensor_copy(memT[0][:], mem_in[:]).then_inc(mem_hi, 1)
                        split_low(mem_in[:], memT, mem_hi, g + 1, mem_split)
                    if attn_ and t == 1:
                        set_values(i, 1)
                    if attn_:
                        for k in range(CHUNKS):
                            if t == INVERT_TICKS[k] and k not in (4, 5):
                                invert_sums(i, k)
                    if norm and t == 5:
                        dve.wait_ge(x_loaded, 16 * (i + 3))
                        layer_norm_stats(i + 2, x_in, stats1, mv1, var1, nhalf1, half1, rstd1,
                                         (ln1_stats, ln1_mean, ln1_var, ln1_half, ln1_seed))
                    if out_ and t == 8:
                        inverse_root(i - 1)
                        layer_norm_apply(i - 1, resid, mv2, rstd2, ln2_rstd, xhat2, z_turned, ln2_ready)
                    if out_ and t == 2:
                        g = i - 1
                        dve.wait_ge(attended, GB * (g + 1))
                        if later(g):
                            dve.wait_ge(proj_ready, g)
                        dve.tensor_copy(attnT[0][:], value_tiles).then_inc(attnT_hi, 1)
                        split_low(value_tiles, attnT, attnT_hi, g + 1, attnT_split)
                    if ffn and t in HIDDEN_TICKS:
                        g, n = i - 2, HIDDEN_TICKS.index(t)
                        dve.wait_ge(hid_relu, HJ * g + n + 1)
                        if n == 0 and later(g):
                            dve.wait_ge(down_ready, g)
                        dve.tensor_copy(hT[0][:, 2 * n:2 * n + 2, :], hid[:, n % 2]).then_inc(hid_hi, 1)
                        if n == HJ - 1:
                            dve.wait_ge(hid_hi, HJ * (g + 1))
                            dve.wait_ge(hid_split, HJ * g + n)
                            dve.tensor_tensor(hT[1][:, 2 * n:2 * n + 2, :], hid[:, n % 2],
                                              hT[0][:, 2 * n:2 * n + 2, :], ALU.subtract
                                              ).then_inc(hid_split, 1)
                    if is_at(i, -1) and t == 3:
                        dve.wait_ge(shift_added, 3)
                    if front and t == 3:
                        g = i + 1
                        dve.wait_ge(q_high, g + 1)
                        for k in range(KT):
                            last = dve.scalar_tensor_tensor(
                                out=q[1][:, k, :], in0=by_tile[1][:, k, :], scalar=bqc[:, k:k + 1],
                                in1=q[0][:, k, :], op0=ALU.add, op1=ALU.subtract)
                        last.then_inc(q_split, 1)
                    if front and t == 5:
                        g = i + 1
                        dve.wait_ge(k_copied, g + 1)
                        if later(g):
                            dve.wait_ge(scores_ready, CHUNKS * i + CPB)
                        for e in range(2):
                            last = dve.tensor_scalar(kk[0][:, :, e, :], k_full[:], par[:, e:e + 1], None,
                                                     ALU.mult)
                        last.then_inc(k_high, 1)
                        dve.wait_ge(k_high, g + 1)
                        for e in range(2):
                            last = dve.scalar_tensor_tensor(
                                out=kk[1][:, :, e, :], in0=k_full[:], scalar=par[:, e:e + 1],
                                in1=kk[0][:, :, e, :], op0=ALU.mult, op1=ALU.subtract)
                        last.then_inc(k_split, 1)
                    if attn_ and t == INVERT_TICKS[4]:
                        invert_sums(i, 4)
                    if front and t == 10:
                        set_values(i + 1, 0)
                    if front and t == 9:
                        if later(i + 1):
                            dve.wait_ge(scores_masked, CHUNKS * (i + 1))
                        dve.wait_ge(mask_loaded, 16 * (i + 2))
                        dve.tensor_scalar(mask_bias[:], mask_in[:], 1.0, -MASKED, ALU.subtract, ALU.mult
                                          ).then_inc(bias_ready, 1)
                    if is_at(i, -2) and t == 10:
                        fold_and_split("q")
                    if norm and t == 10:
                        layer_norm_apply(i + 2, x_in, mv1, rstd1, ln1_rstd, xhat, x_turned, ln1_ready)

            run(dve, iteration, after_first=keys_and_values, after_second=low_parts)

        @block.gpsimd
        def _(pool):
            pool.memset(c1_5[:], 1.5).then_inc(c1_5_set, 1)
            pool.wait_ge(c1_5_set, 1)
            pool.memset(q_stack[96:P].rearrange("p r k n -> p (r k n)").bitcast(F32), 0.0
                        ).then_inc(zeros_set, 1)
            pool.wait_ge(zeros_set, 1)
            pool.memset(k_stack[96:P].rearrange("p r k e s -> p (r k e s)").bitcast(F32), 0.0
                        ).then_inc(zeros_set, 1)
            pool.wait_ge(zeros_set, 2)

            def inverse_root(g):
                pool.wait_ge(ln1_seed, g + 1)
                steps = (4 * NEWTON_STEPS - 1) * g
                for n in range(NEWTON_STEPS):
                    if n:
                        pool.wait_ge(ln1_step, steps + 4 * n)
                    pool.tensor_tensor(newton1[:], rstd1[:], rstd1[:], ALU.mult).then_inc(ln1_step, 1)
                    pool.wait_ge(ln1_step, steps + 4 * n + 1)
                    pool.tensor_tensor(newton1[:], newton1[:], nhalf1[:], ALU.mult).then_inc(ln1_step, 1)
                    pool.wait_ge(ln1_step, steps + 4 * n + 2)
                    pool.tensor_tensor(newton1[:], newton1[:], c1_5[:], ALU.add).then_inc(ln1_step, 1)
                    pool.wait_ge(ln1_step, steps + 4 * n + 3)
                    last = pool.tensor_tensor(rstd1[:], rstd1[:], newton1[:], ALU.mult)
                    last.then_inc(ln1_step if n < NEWTON_STEPS - 1 else ln1_rstd, 1)

            def iteration(i, norm, front, attn_, out_, ffn):
                for t in range(TICKS):
                    if attn_ and t in NORM_TICKS:
                        k = NORM_TICKS.index(t)
                        pool.wait_ge(sums_inverted, CHUNKS * i + k + 1)
                        pool.tensor_tensor(scores[:, k], scores[:, k],
                                           sum_inv[:, k, :].unsqueeze(2).broadcast_to([P, CH, S]),
                                           ALU.mult).then_inc(probs_normed, 1)
                    if ffn and t in HIDDEN_TICKS[:HJ - 1]:
                        g, n = i - 2, HIDDEN_TICKS.index(t)
                        pool.wait_ge(hid_hi, HJ * g + n + 1)
                        pool.tensor_tensor(hT[1][:, 2 * n:2 * n + 2, :], hid[:, n % 2],
                                           hT[0][:, 2 * n:2 * n + 2, :], ALU.subtract
                                           ).then_inc(hid_split, 1)
                    if norm and t == 8:
                        inverse_root(i + 2)
                    if out_ and t == 4:
                        if is_at(i, 1):
                            pool.wait_ge(rows_summed, 1)
                        pool.wait_ge(xres_loaded, 16 * i)
                        pool.tensor_tensor(x_res[:], x_res[:],
                                           bow[:, :].unsqueeze(1).broadcast_to([P, GB, D]),
                                           ALU.add).then_inc(xres_biased, 1)
                    if ffn and t == 2:
                        g = i - 2
                        pool.wait_ge(resid_ready, g + 1)
                        if later(g):
                            pool.wait_ge(y_summed, g)
                        pool.tensor_tensor(resid_b2[:], resid[:],
                                           b2w[:, :].unsqueeze(1).broadcast_to([P, GB, D]),
                                           ALU.add).then_inc(resid_biased, 1)

            run(pool, iteration)

        @block.tensor
        def _(pe):
            def shift_product(name):
                k = KT
                src, shift = SETUP[name][0], (be2c if name == "1" else be1c)
                view = raw(name).rearrange("p (k n) -> p k n", k=k)
                dst = SHIFTS_AT[name]
                pe.wait_ge(weight_loaded[name], 16)
                if name == "v":
                    pe.wait_ge(be1w_set, 1)
                    for j in range(k):
                        last = pe.matmul(dst, be1w[:, j, :], view[:, j, :],
                                         start=(j == 0), stop=(j == k - 1))
                else:
                    for m in range(src.shape[1] // P):
                        for j in range(k):
                            last = pe.matmul(dst[:, m:m + 1], view[:, j, m * P:(m + 1) * P],
                                             shift[:, j:j + 1], start=(j == 0), stop=(j == k - 1))
                last.then_inc(shift_ready, 1)

            def product(dst, pairs, start=True, stop=True, **more):
                n = len(pairs)
                for j, (lhs, rhs) in enumerate(pairs):
                    pe.matmul(dst, lhs[1], rhs[0], start=start and j == 0, stop=False, **more)
                    pe.matmul(dst, lhs[0], rhs[1], start=False, stop=False, **more)
                    last = pe.matmul(dst, lhs[0], rhs[0], start=False, stop=stop and j == n - 1, **more)
                return last

            def cut(pair, *at):
                return pair[0][at], pair[1][at]

            ALL = slice(None)

            def seq(b):
                return slice(b * S, (b + 1) * S)

            def turn(dst, src):
                for k in range(KT):
                    for b in range(GB):
                        last = pe.transpose(dst[:, k, seq(b)], src[:, b, k * P:(k + 1) * P], ident[:])
                return last

            def up(i, t):
                g, n = i - 2, UP_TICKS.index(t)
                if is_at(i, 2) and n == 0:
                    pe.wait_ge(split_lo, SPLIT_AT["2"])
                if n == 0:
                    pe.wait_ge(z_split, g + 1)
                    if later(g):
                        pe.wait_ge(y_summed, g)
                else:
                    pe.wait_ge(hid_relu, HJ * g + n)
                for j in range(2):
                    f = 2 * n + j
                    last = product(ffn_ps[:, j * ROWS:(j + 1) * ROWS],
                                   [(cut(w1, ALL, k, slice(f * P, (f + 1) * P)), cut(zT, ALL, k))
                                    for k in range(KT)])
                last.then_inc(hid_ready, 1)

            def scores_of(i, n):
                b, c = divmod(n, CPB)
                if b == 0:
                    if c == 0:
                        pe.wait_ge(q_stacked, 16 * TERMS * CPB * (i + 1))
                    pe.wait_ge(k_stacked[c], 16 * TERMS * (i + 1))
                if n >= 2 or later(i):
                    pe.wait_ge(scores_masked, CHUNKS * i + n - 1)
                for k in range(KT):
                    last = pe.matmul(score_ps[n % 2][:, k * 2 * S:(k + 1) * 2 * S],
                                     q_stack[:, c, k, seq(b)],
                                     k_stack[:, c, GB * k + b].rearrange("p e s -> p (e s)"),
                                     start=True, stop=True)
                last.then_inc(scores_ready, 1)

            def turn_chunk(g, k):
                pe.wait_ge(probs_normed, CHUNKS * g + k + 1)
                if k >= 2 or later(g):
                    pe.wait_ge(probs_copied, CHUNKS * g + k - 1)
                for h in range(CH):
                    last = pe.transpose(turn_ps[k % 2][:, h * S:(h + 1) * S], scores[:, k, h, :],
                                        ident[:])
                last.then_inc(probs_turned, 1)

            def values_of(g, b):
                pe.wait_ge(probs_copied, CHUNKS * g + CPB * (b + 1))
                pe.wait_ge(values_set, GB * g + b + 1)
                if b == 0 and later(g):
                    pe.wait_ge(attnT_split, g)
                for k in range(KT):
                    for e in range(2):
                        for c in range(CPB):
                            h = 2 * k + e
                            last = pe.matmul(value_tiles[32 * c:32 * (c + 1), k, seq(b)],
                                             v_pad[:, b, head_of(c, h), :],
                                             probs[:, c, h * S:(h + 1) * S], start=(e == 0), stop=(e == 1),
                                             skip_group_check=True)
                last.then_inc(attended, 1)

            def iteration(i, norm, front, attn_, out_, ffn):
                fronts, outs = stages_before(i)
                for t in range(TICKS):
                    if attn_ and t == 0:
                        scores_of(i, 0)
                        scores_of(i, 1)
                    if attn_ and t in SCORE_TICKS:
                        scores_of(i, SCORE_TICKS[t])
                    if attn_ and t == 9:
                        values_of(i, 0)
                    if attn_ and t in TURN_TICKS:
                        turn_chunk(i, TURN_TICKS.index(t))
                    if out_ and t == 0:
                        turn_chunk(i - 1, CHUNKS - 1)
                    if front and t == 0:
                        pe.wait_ge(ln1_ready, i + 2)
                        if not isinstance(i, int) or outs > 0:
                            pe.wait_ge(z_split, outs)
                        turn(by_tile[1], xhat).then_inc(x_turned, 1)
                    if ffn and t in UP_TICKS:
                        up(i, t)
                    if attn_ and t == 1:
                        scores_of(i, 2)
                    if out_ and t == 1:
                        values_of(i - 1, 1)
                    if front and t in (1, 3):
                        which = t // 2
                        if which == 0:
                            pe.wait_ge(x_split, i + 2)
                        elif fronts > 0:
                            pe.wait_ge(values_set, GB * fronts)
                        if is_at(i, -1):
                            pe.wait_ge(split_lo, SPLIT_AT["qk"[which]])
                        for m in range(KT):
                            last = product(by_tile[1 - which][:, m, :],
                                           [(cut((wq, wk)[which], ALL, k, slice(m * P, (m + 1) * P)),
                                             cut(xT, ALL, k)) for k in range(KT)])
                        last.then_inc((q_ready, k_ready)[which], 1)
                    if out_ and t in (5, 6):
                        b = t - 5
                        if is_at(i, 1) and b == 0:
                            pe.wait_ge(split_lo, SPLIT_AT["g"])
                        if b == 0:
                            pe.wait_ge(attnT_split, i)
                            if front:
                                pe.wait_ge(q_split, i + 2)
                            elif outs > 0:
                                pe.wait_ge(z_split, outs)
                            pe.wait_ge(mem_split, i)
                        last = product(by_seq[1][:, b, :],
                                       [(cut(attnT, ALL, k, seq(b)), cut(wo, ALL, k)) for k in range(KT)]
                                       + [(cut(memT, ALL, k, seq(b)), cut(wg, ALL, k)) for k in range(KT)])
                        if b == GB - 1:
                            last.then_inc(proj_ready, 1)
                    if front and t == 8:
                        if is_at(i, -1):
                            pe.wait_ge(split_lo, SPLIT_AT["v"])
                        pe.wait_ge(k_copied, i + 2)
                        for b in range(GB):
                            last = product(by_seq[0][:, b, :],
                                           [(cut(xT, ALL, k, seq(b)), cut(wv, ALL, k)) for k in range(KT)])
                        last.then_inc(v_ready, 1)
                    if out_ and t == 12:
                        pe.wait_ge(ln2_ready, i)
                        pe.wait_ge(resid_ready, i)
                        turn(by_tile[1], xhat2).then_inc(z_turned, 1)
                    if ffn and t in DOWN_TICKS:
                        g, part = i - 2, DOWN_TICKS.index(t)
                        if part == 0:
                            pe.wait_ge(hid_relu, HJ * g + HJ)
                        pe.wait_ge(hid_split, HJ * g + part + 1)
                        for f in range(2 * part, 2 * part + 2):
                            for b in range(GB):
                                last = product(ffn_ps[:, b * D:(b + 1) * D],
                                               [(cut(hT, ALL, f, seq(b)), cut(w2, ALL, f))],
                                               start=(f == 0 and b == 0), stop=(f == FT - 1),
                                               skip_group_check=True)
                        if part == HJ - 1:
                            last.then_inc(down_ready, 1)

            pe.wait_ge(vec_loaded, 16)
            for name in "qkv":
                shift_product(name)
            pe.wait_ge(ident_loaded, 16)
            pe.wait_ge(zeros_set, 2)
            run(pe, iteration, after_second=lambda: shift_product("1"))


def kernel(**inputs):
    import numpy as np
    import concourse.bacc as bacc
    from concourse.bass_utils import run_bass_kernel_spmd

    nc = bacc.Bacc("TRN2", target_bir_lowering=False, num_devices=1)
    arrays, args = {}, []

    def give(name, a):
        arrays[name] = np.ascontiguousarray(a)
        args.append(nc.dram_tensor(name, arrays[name].shape, mybir.dt.from_np(arrays[name].dtype),
                                   kind="ExternalInput").ap())

    give("x_dram", inputs["x"])
    give("memory_dram", np.asarray(inputs["ctx_1024"]).reshape(-1, inputs["ctx_1024"].shape[-1]).T)
    give("mask_dram", inputs["mask_BxSxS2_fk0"])
    for n in ("Wq", "Wk", "Wv", "Wo", "Wg", "W1", "W2"):
        wT = np.asarray(inputs[f"L0_xattn_{n}"]).T
        give(f"{n}T_dram", wT)
    rows = np.arange(P) // 16 % 2
    vectors = {"even_odd": np.stack([rows == 0, rows == 1], axis=1).astype(np.float32)}
    for n, cols in VECTORS[:-1]:
        vectors[n] = np.asarray(inputs[f"L0_xattn_{n}"]).reshape(cols, P).T
    give("vectors_dram", np.concatenate([vectors[n] for n, _ in VECTORS], axis=1))
    give("rows_dram", np.concatenate([np.asarray(inputs[f"L0_xattn_{n}"]) for n in ("bv", "bo", "bg", "b2")]))
    give("identity_dram", np.eye(P, dtype=np.float32))
    shape = tuple(inputs["x"].shape)
    args.append(nc.dram_tensor("out_dram", shape, F32, kind="ExternalOutput").ap())
    xattn_block(nc, *args)
    r = run_bass_kernel_spmd(nc, [arrays], core_ids=[0])
    return r.results[0]["out_dram"]
```
